# Optimizing a Trainium2 kernel written in Bass

```python
import numpy as np
import jax
import jax.numpy as jnp

def _softmax(x, axis=-1):
    return jax.nn.softmax(x, axis=axis)

def _gelu(x):
    return jax.nn.gelu(x, approximate=True)

def _silu(x):
    return jax.nn.silu(x)

def _sigmoid(x):
    return jax.nn.sigmoid(x)

def _layernorm(x, axis=-1, eps=1e-05):
    m = jnp.mean(x, axis=axis, keepdims=True)
    v = jnp.var(x, axis=axis, keepdims=True)
    return (x - m) / jnp.sqrt(v + eps)

def _scatter_add(tgt, idx, src, axis=0):
    return tgt.at[idx].add(src)

def _segment_sum(src, seg, n):
    return jax.ops.segment_sum(src, seg, n)
kernel_name = 'mk_macaron_d1_jaxref_r8_68ff08'

def setup_inputs(seed: int=0):
    np.random.seed(seed)
    _w = jnp.asarray

    def _L0_attn_setup():
        import jax, jax.numpy as jnp
        import numpy as np
        D_MODEL = 128
        N_HEADS = 16
        D_K = D_MODEL // N_HEADS
        THETA = 10000.0

        def _rope(x, pos):
            half = D_K // 2
            inv_freq = THETA ** (-jnp.arange(0, half, dtype=jnp.float32) * 2.0 / D_K)
            ang = pos[:, None].astype(jnp.float32) * inv_freq[None, :]
            cos, sin = (jnp.cos(ang), jnp.sin(ang))
            x1, x2 = (x[..., 0::2], x[..., 1::2])
            r1 = x1 * cos - x2 * sin
            r2 = x1 * sin + x2 * cos
            out = jnp.stack([r1, r2], axis=-1).reshape(x.shape)
            return out
        key = jax.random.key(seed)
        ks = jax.random.split(key, 5)
        b, s = (4, 256)
        sc = 1.0 / np.sqrt(D_MODEL)
        return {'x': jax.random.normal(ks[0], (b, s, D_MODEL), dtype=jnp.float32), 'Wq': jax.random.normal(ks[1], (D_MODEL, D_MODEL), dtype=jnp.float32) * sc, 'Wk': jax.random.normal(ks[2], (D_MODEL, D_MODEL), dtype=jnp.float32) * sc, 'Wv': jax.random.normal(ks[3], (D_MODEL, D_MODEL), dtype=jnp.float32) * sc, 'Wo': jax.random.normal(ks[4], (D_MODEL, D_MODEL), dtype=jnp.float32) * sc}
    _L0_attn_in = _L0_attn_setup()

    def _L0_ffn_setup():
        import jax, jax.numpy as jnp
        import numpy as np
        B, S, D, F, E = (4, 256, 128, 512, 8)
        LN_EPS = 1e-05
        key = jax.random.key(seed)
        ks = jax.random.split(key, 6)
        sc = 0.02
        return {'x': jax.random.normal(ks[0], (B, S, D), dtype=jnp.float32), 'Wr': jax.random.normal(ks[1], (D, E), dtype=jnp.float32) * sc, 'br': jnp.zeros((E,), jnp.float32), 'ln_g': jnp.ones((D,), jnp.float32), 'ln_b': jnp.zeros((D,), jnp.float32), 'W1': jax.random.normal(ks[2], (E, D, F), dtype=jnp.float32) * sc, 'b1': jnp.zeros((E, F), jnp.float32), 'W2': jax.random.normal(ks[3], (E, F, D), dtype=jnp.float32) * sc, 'b2': jnp.zeros((E, D), jnp.float32)}
    _L0_ffn_in = _L0_ffn_setup()
    _d = {'L0_attn_x': _L0_attn_in['x'], 'L0_attn_Wq': _L0_attn_in['Wq'], 'L0_attn_Wk': _L0_attn_in['Wk'], 'L0_attn_Wv': _L0_attn_in['Wv'], 'L0_attn_Wo': _L0_attn_in['Wo'], 'L0_ffn_Wr': _L0_ffn_in['Wr'], 'L0_ffn_br': _L0_ffn_in['br'], 'L0_ffn_ln_g': _L0_ffn_in['ln_g'], 'L0_ffn_ln_b': _L0_ffn_in['ln_b'], 'L0_ffn_W1': _L0_ffn_in['W1'], 'L0_ffn_b1': _L0_ffn_in['b1'], 'L0_ffn_W2': _L0_ffn_in['W2'], 'L0_ffn_b2': _L0_ffn_in['b2']}
    _x0 = _d['L0_attn_x']
    _d['L0_attn_x'] = jax.random.normal(jax.random.fold_in(jax.random.key(seed), 1), (4, 1024, 128), dtype=_x0.dtype)
    del _x0
    return _d

def reference(L0_attn_x, L0_attn_Wq, L0_attn_Wk, L0_attn_Wv, L0_attn_Wo, L0_ffn_Wr, L0_ffn_br, L0_ffn_ln_g, L0_ffn_ln_b, L0_ffn_W1, L0_ffn_b1, L0_ffn_W2, L0_ffn_b2):

    def _L0_attn_ref(x, Wq, Wk, Wv, Wo):
        import jax, jax.numpy as jnp
        import numpy as np
        D_MODEL = 128
        N_HEADS = 16
        D_K = D_MODEL // N_HEADS
        THETA = 10000.0

        def _rope(x, pos):
            half = D_K // 2
            inv_freq = THETA ** (-jnp.arange(0, half, dtype=jnp.float32) * 2.0 / D_K)
            ang = pos[:, None].astype(jnp.float32) * inv_freq[None, :]
            cos, sin = (jnp.cos(ang), jnp.sin(ang))
            x1, x2 = (x[..., 0::2], x[..., 1::2])
            r1 = x1 * cos - x2 * sin
            r2 = x1 * sin + x2 * cos
            out = jnp.stack([r1, r2], axis=-1).reshape(x.shape)
            return out
        b, s, _ = x.shape
        pos = jnp.arange(s)

        def split_heads(t):
            return t.reshape(b, s, N_HEADS, D_K).transpose(0, 2, 1, 3).reshape(b * N_HEADS, s, D_K)
        q = split_heads(x @ Wq.T)
        k = split_heads(x @ Wk.T)
        v = split_heads(x @ Wv.T)
        q = _rope(q, pos)
        k = _rope(k, pos)
        score = jnp.einsum('bqd,bkd->bqk', q, k)
        causal = jnp.tril(jnp.ones((s, s), dtype=bool))
        score = jnp.where(causal[None], score, -jnp.inf)
        attn = jax.nn.softmax(score / jnp.sqrt(jnp.float32(D_K)), axis=-1)
        out = jnp.einsum('bqk,bkd->bqd', attn, v)
        out = out.reshape(b, N_HEADS, s, D_K).transpose(0, 2, 1, 3).reshape(b, s, D_MODEL)
        return out @ Wo.T

    def _L0_ffn_ref(x, Wr, br, ln_g, ln_b, W1, b1, W2, b2):
        import jax, jax.numpy as jnp
        import numpy as np
        B, S, D, F, E = (4, 256, 128, 512, 8)
        LN_EPS = 1e-05
        tokens_shape = x.shape[:-1]
        xt = x.reshape(-1, x.shape[-1])
        router_logits = xt @ Wr + br
        router_probs = jax.nn.softmax(router_logits, axis=-1)
        gates = jnp.max(router_probs, axis=-1, keepdims=True)
        idx = jnp.argmax(router_probs, axis=-1)
        onehot = jax.nn.one_hot(idx, E, dtype=xt.dtype)
        mu = jnp.mean(xt, axis=-1, keepdims=True)
        var = jnp.mean(jnp.square(xt - mu), axis=-1, keepdims=True)
        xn = (xt - mu) * jax.lax.rsqrt(var + LN_EPS) * ln_g + ln_b
        h = jnp.einsum('te,td,edf->tf', onehot, xn, W1) + b1[idx]
        h = jax.nn.relu(h)
        y = jnp.einsum('te,tf,efd->td', onehot, h, W2) + b2[idx]
        y = y * gates
        return y.reshape(tokens_shape + (y.shape[-1],))
    x = L0_attn_x
    x = x + 0.5 * _L0_ffn_ref(_layernorm(x, axis=-1), L0_ffn_Wr, L0_ffn_br, L0_ffn_ln_g, L0_ffn_ln_b, L0_ffn_W1, L0_ffn_b1, L0_ffn_W2, L0_ffn_b2)
    x = x + _L0_attn_ref(_layernorm(x, axis=-1), L0_attn_Wq, L0_attn_Wk, L0_attn_Wv, L0_attn_Wo)
    x = x + 0.5 * _L0_ffn_ref(_layernorm(x, axis=-1), L0_ffn_Wr, L0_ffn_br, L0_ffn_ln_g, L0_ffn_ln_b, L0_ffn_W1, L0_ffn_b1, L0_ffn_W2, L0_ffn_b2)
    return x

_drawn_inputs = setup_inputs


def setup_inputs(seed=0):
    import zlib

    import numpy as np

    out = dict(_drawn_inputs(seed))
    spreads = {'L0_ffn_br': (0.0, 0.381),
     'L0_ffn_ln_g': (1.0, 0.6),
     'L0_ffn_ln_b': (0.0, 0.8),
     'L0_ffn_b1': (0.0, 0.8),
     'L0_ffn_b2': (0.0, 0.452)}
    factors = {'L0_ffn_Wr': 2.753, 'L0_ffn_W1': 4.869, 'L0_ffn_W2': 3.81}
    for name, (base, spread) in spreads.items():
        noise = np.random.default_rng([zlib.crc32(name.encode()), seed]).standard_normal(out[name].shape)
        drawn = base * np.exp(spread * noise) if base else spread * noise
        out[name] = jnp.asarray(drawn.astype(out[name].dtype))
    for name, factor in factors.items():
        out[name] = (out[name] * factor).astype(out[name].dtype)
    return out
```

```python
from contextlib import ExitStack, contextmanager

import numpy as np

import concourse.bass as bass
from concourse import mybir

F32 = mybir.dt.float32
BF16 = mybir.dt.bfloat16
U32 = mybir.dt.uint32
I32 = mybir.dt.int32
ALU = mybir.AluOpType
ACT = mybir.ActivationFunctionType
AX = mybir.AxisListType

B, S, D = 4, 1024, 128
H, DK = 16, 8
E, F = 8, 512
P = 128
NT = B * S // P
TB = S // P
FB = F // P
NS = NT + E
EPS = 1e-5
SCALE = DK ** -0.5
NEG = -1e30
QH = 4
NST = B * H // QH
RW = QH * DK
KINDS = 3
PR = KINDS * KINDS * DK
MR = KINDS
CH = 512
NCH = S // CH
CB = CH // P
RING = 3

CONST = {}
_at = 0
for _name, _width in (("ident", P), ("before", P), ("mask", P), ("ramp", E), ("full", NT),
                      ("tri", E * E), ("tile", NS), ("cos", S), ("sin", S)):
    CONST[_name] = (_at, _at + _width)
    _at += _width
CONST_W = _at


def constants():
    t = np.zeros((P, CONST_W), np.float32)

    def put(name, a):
        t[:, CONST[name][0]:CONST[name][1]] = a

    i = np.arange(P)
    put("ident", np.eye(P))
    put("before", i[:, None] < i[None, :])
    put("mask", np.where(i[None, :] <= i[:, None], 0.0, NEG))
    put("ramp", np.arange(E, 0, -1))
    put("full", P * np.arange(NT))
    put("tri", (np.arange(E)[None, :] < np.arange(E)[:, None]).reshape(1, -1))
    put("tile", np.arange(NS))
    half = DK // 2
    freq = np.float32(10000.0) ** (-np.arange(0, half, dtype=np.float32) * np.float32(2.0) / np.float32(DK))
    angle = np.arange(S, dtype=np.float32)[None, :] * freq[:, None].astype(np.float32)
    row = (i % DK) // 2
    put("cos", np.cos(angle)[row])
    put("sin", np.sin(angle)[row] * np.where(i % 2 == 0, -1.0, 1.0)[:, None])
    return t


def ds(start, size):
    return bass.ds(start, size)


@contextmanager
def steps(eng, start, end, step):
    with eng.Fori(start // step, end // step) as i:
        yield i * step


def wait(eng, sem, value):
    if isinstance(value, int) and value <= 0:
        return
    eng.wait_ge(sem, value)


class Chain:

    def __init__(self, eng, sem):
        self.eng, self.sem, self.n = eng, sem, 0

    def __call__(self, ins):
        self.n += 1
        ins.then_inc(self.sem, 1)
        self.eng.wait_ge(self.sem, self.n)


class Kept:
    pass


def build(nc, x, WqT, WqsT, WkT, WksT, WvT, WoT, Wr, br, ln_g, ln_b, W1, b1, W2, b2, const, out):
    ctx = ExitStack()
    with ctx:
        def sb(name, shape, dt=F32):
            return ctx.enter_context(nc.sbuf_tensor(name, shape, dt))

        n = Kept()
        n.x, n.WqT, n.WqsT, n.WkT, n.WksT, n.WvT = x, WqT, WqsT, WkT, WksT, WvT
        n.WoT, n.Wr, n.br, n.ln_g, n.ln_b, n.W1 = WoT, Wr, br, ln_g, ln_b, W1
        n.b1, n.W2, n.b2, n.const = b1, W2, b2, const
        n.tok = sb("tok", [P, NT, D])
        n.cst = sb("cst", [P, CONST_W])
        n.identb = sb("identb", [P, P], BF16)
        n.beforeb = sb("beforeb", [P, P], BF16)
        n.maskb = sb("maskb", [P, P], BF16)
        n.onesb = sb("onesb", [P, P], BF16)
        n.wproj = sb("wproj", [P, 6, D])
        n.wr = sb("wr", [P, E])
        n.gb = sb("gb", [P, 2])
        n.brb = sb("brb", [P, E])
        n.w1 = sb("w1", [P, E * F])
        n.w2 = sb("w2", [P, FB, E * D])
        n.b1b = sb("b1b", [P, E * F])
        n.b2b = sb("b2b", [P, E * D])
        n.stats = sb("stats", [P, NT, 6])
        n.mv = sb("mv", [P, NT, 2])
        n.rstd = sb("rstd", [P, NT])
        n.shared = sb("shared", [P, NT, D])
        n.vals = sb("vals", [P, NST, TB, RW])

        n.ks = [sb(f"ks{i}", [PR + MR, QH * S], BF16) for i in range(RING)]
        n.vs = [sb(f"vs{i}", [P, TB, QH, 32]) for i in range(RING)]

        def c(name, rows=P):
            return n.cst[0:rows, CONST[name][0]:CONST[name][1]]

        n.q_dram = nc.dram_tensor("q_split", (KINDS * DK, NCH, B * H, CH), BF16, kind="Internal").ap()
        n.k_dram = nc.dram_tensor("k_split", (KINDS * DK, B * H, S), BF16, kind="Internal").ap()
        n.sort_dram = [nc.dram_tensor(f"sorted{r}", (NS * P, D), F32, kind="Internal").ap() for r in range(2)]
        n.ysort_dram = [nc.dram_tensor(f"ysorted{r}", (NS * P, D), F32, kind="Internal").ap() for r in range(2)]

        n.c = c
        setup(nc, n)
        ffn(nc, n, 0)
        project(nc, n)
        attention(nc, n)
        output_projection(nc, n)
        ffn(nc, n, 1)
        store(nc, n.tok, out)


def setup(nc, n):
    with ExitStack() as ctx:
        zero = ctx.enter_context(nc.sbuf_tensor("zero", [P, 4 * D], F32))
        loaded = ctx.enter_context(nc.semaphore("setup_loaded"))
        const_loaded = ctx.enter_context(nc.semaphore("setup_const_loaded"))
        zeroed = ctx.enter_context(nc.semaphore("setup_zeroed"))
        cleared = ctx.enter_context(nc.semaphore("setup_cleared"))
        block = ctx.enter_context(nc.Block())

        @block.sync
        def _(sp):
            sp.dma_start(n.cst[:, :], n.const).then_inc(const_loaded, 16)
            for b in range(B):
                sp.dma_start(n.tok[:, b * TB:(b + 1) * TB, :],
                             n.x[b].rearrange("(n p) d -> p n d", p=P)).then_inc(loaded, 16)
            for i, w in enumerate((n.WqT, n.WqsT, n.WkT, n.WksT, n.WvT, n.WoT)):
                sp.dma_start(n.wproj[:, i, :], w).then_inc(loaded, 16)
            sp.wait_ge(loaded, 16 * (B + 6 + 7 + FB))

        @block.scalar
        def _(act):
            act.dma_start(n.wr[:, :], n.Wr).then_inc(loaded, 16)
            act.dma_start(n.gb[:, 0:1], n.ln_g.rearrange("(p a) -> p a", a=1)).then_inc(loaded, 16)
            act.dma_start(n.gb[:, 1:2], n.ln_b.rearrange("(p a) -> p a", a=1)).then_inc(loaded, 16)
            act.dma_start(n.brb[:, :], n.br.partition_broadcast(P)).then_inc(loaded, 16)
            act.dma_start(n.w1[:, :].rearrange("p (e f) -> p e f", e=E),
                          n.W1.rearrange("e d f -> d e f")).then_inc(loaded, 16)
            for k in range(FB):
                act.dma_start(n.w2[:, k, :].rearrange("p (e d) -> p e d", e=E),
                              n.W2[:, k * P:(k + 1) * P, :].rearrange("e f d -> f e d")).then_inc(loaded, 16)
            act.dma_start(n.b1b[:, :], n.b1.rearrange("e f -> (e f)").partition_broadcast(P)).then_inc(loaded, 16)
            act.dma_start(n.b2b[:, :], n.b2.rearrange("e d -> (e d)").partition_broadcast(P)).then_inc(loaded, 16)

        @block.gpsimd
        def _(pool):
            nc.gpsimd.memset(zero[:, :], 0.0).then_inc(zeroed, 1)
            pool.wait_ge(zeroed, 1)
            for r in range(2):
                for k in range(NS // 4):
                    pool.dma_start(n.sort_dram[r][k * 4 * P:(k + 1) * 4 * P, :].rearrange("(p a) d -> p (a d)", a=4),
                                   zero[:, :]).then_inc(cleared, 16)
            pool.wait_ge(cleared, 16 * 2 * (NS // 4))

        @block.vector
        def _(dve):
            nc.vector.memset(n.onesb[:, :], 1.0)
            for r in range(RING):
                nc.vector.memset(n.ks[r][64:PR + MR, :], 1.0)
                nc.vector.memset(n.vs[r][:, :, :, DK + 1:], 0.0)
                nc.vector.memset(n.vs[r][:, :, :, DK:DK + 1], 1.0)
            dve.wait_ge(const_loaded, 16)
            nc.vector.tensor_copy(n.identb[:, :], n.c("ident"))
            nc.vector.tensor_copy(n.beforeb[:, :], n.c("before"))
            nc.vector.tensor_copy(n.maskb[:, :], n.c("mask"))


def store(nc, tok, out):
    with ExitStack() as ctx:
        stored = ctx.enter_context(nc.semaphore("stored"))
        block = ctx.enter_context(nc.Block())

        @block.sync
        def _(sp):
            for b in range(B):
                sp.dma_start(out[b].rearrange("(n p) d -> p n d", p=P),
                             tok[:, b * TB:(b + 1) * TB, :]).then_inc(stored, 16)
            sp.wait_ge(stored, 16 * B)


def token_stats(nc, dve, n, stat_done, link):
    with steps(dve, 0, NT, 4) as t:
        for k in range(4):
            nc.vector.bn_stats(n.stats[:, ds(t + k, 1), :], n.tok[:, ds(t + k, 1), :]).then_inc(stat_done, 1)
    dve.wait_ge(stat_done, NT)
    mean, var = n.mv[:, :, 0], n.mv[:, :, 1]
    even, odd, sq_even, sq_odd = (n.stats[:, :, k] for k in (1, 4, 2, 5))
    link(nc.vector.tensor_tensor(mean, even, odd, ALU.add))
    link(nc.vector.tensor_scalar(mean, mean, 0.5, None, ALU.mult))
    link(nc.vector.tensor_tensor(var, sq_even, sq_odd, ALU.add))
    link(nc.vector.tensor_tensor(even, even, odd, ALU.subtract))
    link(nc.vector.scalar_tensor_tensor(even, even, 0.25, even, ALU.mult, ALU.mult))
    link(nc.vector.scalar_tensor_tensor(var, var, 1.0 / D, even, ALU.mult, ALU.add))


def rsqrt(nc, dve, link, out, var, shifted, root, corr, square_ready, root_ready, turn):
    nc.vector.tensor_scalar(shifted[:, :], var, EPS, None, ALU.add).then_inc(square_ready, 1)
    dve.wait_ge(root_ready, turn)
    link(nc.vector.reciprocal(out[:, :], root[:, :]))
    link(nc.vector.tensor_tensor(corr[:, :], out[:, :], out[:, :], ALU.mult))
    link(nc.vector.tensor_tensor(corr[:, :], corr[:, :], shifted[:, :], ALU.mult))
    link(nc.vector.tensor_scalar(corr[:, :], corr[:, :], -0.5, 1.5, ALU.mult, ALU.add))
    link(nc.vector.tensor_tensor(out[:, :], out[:, :], corr[:, :], ALU.mult))


def root_of(nc, act, root, shifted, square_ready, root_ready, turn):
    act.wait_ge(square_ready, turn)
    nc.scalar.activation(root[:, :], shifted[:, :], ACT.Sqrt).then_inc(root_ready, 1)


def ffn(nc, n, r):
    NCHK = NT // 4
    outer = ExitStack()
    with outer:
        def sb(name, shape, dt=F32):
            return outer.enter_context(nc.sbuf_tensor(f"f{r}_{name}", shape, dt))

        pos = sb("pos", [P, NT], U32)
        half_gate = sb("half_gate", [P, NT])
        tile_expert = sb("tile_expert", [1, NS], I32)
        small = [sb(f"small{i}", [P, NT]) for i in range(6)]
        lg = [sb(f"lg{i}", [P, NT, E]) for i in range(3)]
        onehot = sb("onehot", [P, NT, E], BF16)
        cnt = sb("cnt", [P, E])
        ntile = sb("ntile", [P, E])
        first = sb("first", [P, E])
        xT = [sb(f"xT{i}", [P, 4 * P]) for i in range(2)]
        te = [sb(f"te{i}", [1, NS, E]) for i in range(1)]
        tef = sb("tef", [1, NS])

        with ExitStack() as ctx:
            def sem(name):
                return ctx.enter_context(nc.semaphore(f"f{r}_{name}"))

            psT = [ctx.enter_context(nc.psum_tensor(f"f{r}_psT{i}", [P, 512], F32)) for i in range(2)]
            psL = ctx.enter_context(nc.psum_tensor(f"f{r}_psL", [P, NT, E], F32))
            psR = ctx.enter_context(nc.psum_tensor(f"f{r}_psR", [P, NT, E], F32))
            psC = ctx.enter_context(nc.psum_tensor(f"f{r}_psC", [P, E], F32))
            stat_done, chain = sem("stat_done"), sem("chain")
            square_ready, root_ready = sem("square_ready"), sem("root_ready")
            normed, turned, turned_copied, logits_done = (sem("normed"), sem("turned"), sem("turned_copied"),
                                                          sem("logits_done"))
            shifted, exp_done, onehot_ready, ranks_done = (sem("shifted"), sem("exp_done"), sem("onehot_ready"),
                                                           sem("ranks_done"))
            pos_ready, scattered, ranks_read = sem("pos_ready"), sem("scattered"), sem("ranks_read")
            block = ctx.enter_context(nc.Block())

            @block.vector
            def _(dve):
                link = Chain(dve, chain)
                token_stats(nc, dve, n, stat_done, link)
                rstd_u, scale, inv_u, shift, root, corr = small
                rsqrt(nc, dve, link, n.rstd, n.mv[:, :, 1], shift, root, corr, square_ready, root_ready, 1)
                link(nc.vector.tensor_tensor(scale[:, :], n.rstd[:, :], n.rstd[:, :], ALU.mult))
                link(nc.vector.tensor_tensor(scale[:, :], scale[:, :], n.mv[:, :, 1], ALU.mult))
                rsqrt(nc, dve, link, rstd_u, scale[:, :], shift, root, corr, square_ready, root_ready, 2)
                link(nc.vector.tensor_tensor(inv_u[:, :], shift[:, :], rstd_u[:, :], ALU.mult))
                link(nc.vector.tensor_tensor(scale[:, :], n.rstd[:, :], rstd_u[:, :], ALU.mult))
                with steps(dve, 0, NT, 4) as t:
                    for k in range(4):
                        nc.vector.tensor_scalar(n.shared[:, ds(t + k, 1), :], n.tok[:, ds(t + k, 1), :],
                                                n.mv[:, ds(t + k, 1), 0], scale[:, ds(t + k, 1)],
                                                ALU.subtract, ALU.mult).then_inc(normed, 1)
                logit, other, rank = lg
                dve.wait_ge(logits_done, NT)
                link(nc.vector.tensor_tensor(logit[:, :, :], psL[:, :, :],
                                             inv_u[:, :].unsqueeze(2).to_broadcast([P, NT, E]), ALU.mult))
                link(nc.vector.tensor_tensor(logit[:, :, :], logit[:, :, :],
                                             n.brb[:, :].unsqueeze(1).to_broadcast([P, NT, E]), ALU.add))
                top, pick = small[4], small[5]
                link(nc.vector.reduce_max(top[:, :], logit[:, :, :], AX.X))
                topb = top[:, :].unsqueeze(2).to_broadcast([P, NT, E])
                link(nc.vector.tensor_tensor(other[:, :, :], logit[:, :, :], topb, ALU.is_equal))
                rampb = n.c("ramp").unsqueeze(1).to_broadcast([P, NT, E])
                link(nc.vector.tensor_tensor(other[:, :, :], other[:, :, :], rampb, ALU.mult))
                link(nc.vector.reduce_max(pick[:, :], other[:, :, :], AX.X))
                nc.vector.tensor_tensor(onehot[:, :, :], pick[:, :].unsqueeze(2).to_broadcast([P, NT, E]),
                                        rampb, ALU.is_equal).then_inc(onehot_ready, 1)
                nc.vector.tensor_tensor(logit[:, :, :], logit[:, :, :], topb, ALU.subtract).then_inc(shifted, 1)
                dve.wait_ge(ranks_done, 2)
                link(nc.vector.tensor_copy(cnt[:, :], psC[:, :]))
                wide = other[:, :, :].rearrange("p n e -> p (n e)").rearrange("p (e n) -> p e n", e=E)
                link(nc.vector.tensor_tensor(wide, cnt[:, :].unsqueeze(2).to_broadcast([P, E, NT]),
                                             n.c("full").unsqueeze(1).to_broadcast([P, E, NT]), ALU.is_gt))
                link(nc.vector.reduce_sum(ntile[:, :], wide, AX.X))
                tri = other[:, 0:E, :]
                link(nc.vector.tensor_tensor(tri, n.c("tri").rearrange("p (a b) -> p a b", a=E),
                                             ntile[:, :].unsqueeze(1).to_broadcast([P, E, E]), ALU.mult))
                link(nc.vector.reduce_sum(first[:, :], tri, AX.X))
                link(nc.vector.scalar_tensor_tensor(rank[:, :, :],
                                                    first[:, :].unsqueeze(1).to_broadcast([P, NT, E]), float(P),
                                                    psR[:, :, :], ALU.mult, ALU.add))
                link(nc.vector.tensor_tensor(rank[:, :, :], rank[:, :, :], onehot[:, :, :], ALU.mult))
                link(nc.vector.reduce_sum(pick[:, :], rank[:, :, :], AX.X))
                nc.vector.tensor_copy(pos[:, :], pick[:, :]).then_inc(pos_ready, 1)
                link(nc.vector.tensor_tensor(first[:, :], first[:, :], ntile[:, :], ALU.add))
                link(nc.vector.tensor_tensor(te[0][:, :, :], first[0:1, :].unsqueeze(1).to_broadcast([1, NS, E]),
                                             n.c("tile", 1).unsqueeze(2).to_broadcast([1, NS, E]), ALU.is_le))
                link(nc.vector.reduce_sum(tef[:, :], te[0][:, :, :], AX.X))
                link(nc.vector.tensor_scalar(tef[:, :], tef[:, :], float(E - 1), None, ALU.min))
                link(nc.vector.tensor_copy(tile_expert[:, :], tef[:, :]))
                dve.wait_ge(exp_done, 1)
                link(nc.vector.reduce_sum(top[:, :], logit[:, :, :], AX.X))
                link(nc.vector.reciprocal(top[:, :], top[:, :]))
                link(nc.vector.tensor_scalar(half_gate[:, :], top[:, :], 0.5, None, ALU.mult))

            @block.tensor
            def _(pe):
                def router(g):
                    pe.wait_ge(turned_copied, g + 1)
                    for k in range(4):
                        nc.tensor.matmul(psL[:, 4 * g + k, :], xT[g % 2][:, k * P:(k + 1) * P], n.wr[:, :],
                                         start=True, stop=True).then_inc(logits_done, 1)

                for g in range(NCHK):
                    if g >= 2:
                        pe.wait_ge(turned_copied, g - 1)
                    for k in range(4):
                        pe.wait_ge(normed, 4 * g + k + 1)
                        nc.tensor.transpose(psT[g % 2][:, k * P:(k + 1) * P], n.shared[:, 4 * g + k, :],
                                            n.c("ident")).then_inc(turned, 1)
                    if g >= 1:
                        router(g - 1)
                router(NCHK - 1)
                pe.wait_ge(onehot_ready, 1)
                nc.tensor.matmul(psR[:, :, :], n.beforeb[:, :], onehot[:, :, :], start=True, stop=False)
                for k in range(1, NT):
                    last = nc.tensor.matmul(psR[:, k:NT, :], n.onesb[:, :], onehot[:, 0:NT - k, :],
                                            start=False, stop=(k == NT - 1))
                last.then_inc(ranks_done, 1)
                for k in range(NT):
                    last = nc.tensor.matmul(psC[:, :], n.onesb[:, :], onehot[:, k, :],
                                            start=(k == 0), stop=(k == NT - 1))
                last.then_inc(ranks_done, 1)

            @block.scalar
            def _(act):
                for turn in (1, 2):
                    root_of(nc, act, small[4], small[3], square_ready, root_ready, turn)
                for g in range(NCHK):
                    act.wait_ge(turned, 4 * (g + 1))
                    if g >= 2:
                        act.wait_ge(logits_done, 4 * (g - 1))
                    nc.scalar.activation(xT[g % 2][:, :], psT[g % 2][:, :], ACT.Copy).then_inc(turned_copied, 1)
                act.wait_ge(shifted, 1)
                nc.scalar.activation(lg[0][:, :, :], lg[0][:, :, :], ACT.Exp).then_inc(exp_done, 1)

            @block.gpsimd
            def _(pool):
                pool.wait_ge(pos_ready, 1)
                pool.wait_ge(normed, NT)
                for t in range(NT):
                    pool.indirect_dma_start(
                        out=n.sort_dram[r][:, :],
                        out_offset=bass.IndirectOffsetOnAxis(ap=pos[:, t:t + 1], axis=0),
                        in_=n.shared[:, t, :], in_offset=None).then_inc(scattered, 16)
                pool.wait_ge(scattered, 16 * NT)

        with ExitStack() as ctx:
            def sem(name):
                return ctx.enter_context(nc.semaphore(f"g{r}_{name}"))

            def psum(name, width=512):
                return ctx.enter_context(nc.psum_tensor(f"g{r}_{name}", [P, width], F32))

            xs = [ctx.enter_context(nc.sbuf_tensor(f"g{r}_xs{i}", [P, D], F32)) for i in range(4)]
            xsT = [ctx.enter_context(nc.sbuf_tensor(f"g{r}_xsT{i}", [P, P], F32)) for i in range(2)]
            hid = [ctx.enter_context(nc.sbuf_tensor(f"g{r}_hid{i}", [P, F], F32)) for i in range(2)]
            hidT = [ctx.enter_context(nc.sbuf_tensor(f"g{r}_hidT{i}", [P, F], F32)) for i in range(2)]
            ys = [ctx.enter_context(nc.sbuf_tensor(f"g{r}_ys{i}", [P, D], F32)) for i in range(4)]
            psX = [psum("psX0", P), psum("psX1", P)]
            psH, psHT = [psum("psH0"), psum("psH1")], [psum("psHT0"), psum("psHT1")]
            psY = [psum("psY0", P), psum("psY1", P)]
            loaded = [sem(f"loaded{i}") for i in range(4)]
            x_turned, x_ready, h_done, h_ready, h_turned, ht_ready, y_done, y_ready, gathered, added = (
                sem(k) for k in ("x_turned", "x_ready", "h_done", "h_ready", "h_turned", "ht_ready", "y_done",
                                 "y_ready", "gathered", "added"))
            y_stored = [sem(f"y_stored{i}") for i in range(4)]
            block = ctx.enter_context(nc.Block())

            @block.sync
            def _(sp):
                def load(t, k):
                    sp.dma_start(xs[k][:, :], n.sort_dram[r][ds(t * P, P), :]).then_inc(loaded[k], 16)

                for k in range(4):
                    load(k, k)
                with steps(sp, 4, NS, 4) as t:
                    for k in range(4):
                        sp.wait_ge(x_turned, t + k - 3)
                        load(t + k, k)

            @block.tensor
            def _(pe):
                def turn_x(t, k, reg=True):
                    pe.wait_ge(loaded[k], (t - k) * 4 + 16)
                    wait(pe, x_ready, t - 1)
                    nc.tensor.transpose(psX[k % 2][:, :], xs[k][:, :], n.c("ident")).then_inc(x_turned, 1)

                def hidden(t, k):
                    e = pe.value_load(tile_expert[0:1, ds(t, 1)], min_val=0, max_val=E - 1)
                    pe.wait_ge(x_ready, t + 1)
                    wait(pe, h_ready, t - 1)
                    nc.tensor.matmul(psH[k % 2][:, :], xsT[k % 2][:, :], n.w1[:, ds(e * F, F)],
                                     start=True, stop=True).then_inc(h_done, 1)

                def turn_h(t, k):
                    pe.wait_ge(h_ready, t + 1)
                    wait(pe, ht_ready, t - 1)
                    for f in range(FB):
                        last = nc.tensor.transpose(psHT[k % 2][:, f * P:(f + 1) * P],
                                                   hid[k % 2][:, f * P:(f + 1) * P], n.c("ident"))
                    last.then_inc(h_turned, 1)

                def result(t, k):
                    e = pe.value_load(tile_expert[0:1, ds(t, 1)], min_val=0, max_val=E - 1)
                    pe.wait_ge(ht_ready, t + 1)
                    wait(pe, y_ready, t - 1)
                    for f in range(FB):
                        last = nc.tensor.matmul(psY[k % 2][:, :], hidT[k % 2][:, f * P:(f + 1) * P],
                                                n.w2[:, f, ds(e * D, D)], start=(f == 0), stop=(f == FB - 1))
                    last.then_inc(y_done, 1)

                def step(t, k):
                    hidden(t, k)
                    turn_x(t + 1, (k + 1) % 4)
                    turn_h(t - 1, (k - 1) % 4)
                    result(t - 2, (k - 2) % 4)

                turn_x(0, 0)
                hidden(0, 0)
                turn_x(1, 1)
                hidden(1, 1)
                turn_x(2, 2)
                turn_h(0, 0)
                step(2, 2)
                step(3, 3)
                with steps(pe, 4, NS - 4, 4) as t:
                    for k in range(4):
                        step(t + k, k)
                for t in range(NS - 4, NS - 1):
                    step(t, t % 4)
                hidden(NS - 1, 3)
                turn_h(NS - 2, 2)
                result(NS - 3, 1)
                turn_h(NS - 1, 3)
                result(NS - 2, 2)
                result(NS - 1, 3)

            @block.scalar
            def _(act):
                def x_copy(t, k):
                    act.wait_ge(x_turned, t + 1)
                    wait(act, h_done, t - 1)
                    nc.scalar.activation(xsT[k % 2][:, :], psX[k % 2][:, :], ACT.Identity,
                                         bias=n.gb[:, 1:2], scale=n.gb[:, 0:1]).then_inc(x_ready, 1)

                def h_copy(t, k):
                    act.wait_ge(h_turned, t + 1)
                    wait(act, y_done, t - 1)
                    nc.scalar.activation(hidT[k % 2][:, :], psHT[k % 2][:, :], ACT.Relu).then_inc(ht_ready, 1)

                x_copy(0, 0)
                x_copy(1, 1)
                x_copy(2, 2)
                h_copy(0, 0)
                x_copy(3, 3)
                h_copy(1, 1)
                with steps(act, 4, NS, 4) as t:
                    for k in range(4):
                        x_copy(t + k, k)
                        h_copy(t + k - 2, (k - 2) % 4)
                h_copy(NS - 2, 2)
                h_copy(NS - 1, 3)

            @block.vector
            def _(dve):
                def h_bias(t, k):
                    e = dve.value_load(tile_expert[0:1, ds(t, 1)], min_val=0, max_val=E - 1)
                    dve.wait_ge(h_done, t + 1)
                    wait(dve, h_turned, t - 1)
                    nc.vector.tensor_tensor(hid[k % 2][:, :], psH[k % 2][:, :], n.b1b[:, ds(e * F, F)],
                                            ALU.add).then_inc(h_ready, 1)

                def y_bias(t, k):
                    e = dve.value_load(tile_expert[0:1, ds(t, 1)], min_val=0, max_val=E - 1)
                    dve.wait_ge(y_done, t + 1)
                    if not (isinstance(t, int) and t < 4):
                        dve.wait_ge(y_stored[k], (t - k) * 4)
                    nc.vector.tensor_tensor(ys[k][:, :], psY[k % 2][:, :], n.b2b[:, ds(e * D, D)],
                                            ALU.add).then_inc(y_ready, 1)

                for t in range(6):
                    h_bias(t, t % 4)
                    if t >= 2:
                        y_bias(t - 2, (t - 2) % 4)
                with steps(dve, 4, NS - 4, 4) as t:
                    for k in range(4):
                        h_bias(t + k + 2, (k + 2) % 4)
                        y_bias(t + k, k)
                for t in range(NS - 4, NS):
                    if t + 2 < NS:
                        h_bias(t + 2, (t + 2) % 4)
                    y_bias(t, t % 4)
                dve.wait_ge(gathered, 16 * NT)
                for t in range(NT):
                    nc.vector.scalar_tensor_tensor(n.tok[:, t, :], n.shared[:, t, :], half_gate[:, t:t + 1],
                                                   n.tok[:, t, :], ALU.mult, ALU.add)

            @block.gpsimd
            def _(pool):
                def keep(t, k):
                    pool.wait_ge(y_ready, t + 1)
                    pool.dma_start(n.ysort_dram[r][ds(t * P, P), :], ys[k][:, :]).then_inc(y_stored[k], 16)

                with steps(pool, 0, NS, 4) as t:
                    for k in range(4):
                        keep(t + k, k)
                for k in range(4):
                    pool.wait_ge(y_stored[k], 16 * (NS // 4))
                for t in range(NT):
                    pool.indirect_dma_start(
                        out=n.shared[:, t, :], out_offset=None, in_=n.ysort_dram[r][:, :],
                        in_offset=bass.IndirectOffsetOnAxis(ap=pos[:, t:t + 1], axis=0)).then_inc(gathered, 16)
                pool.wait_ge(gathered, 16 * NT)


def project(nc, n):
    NC8 = B * NCH
    QB = H // QH
    with ExitStack() as ctx:
        def sb(name, shape, dt=F32):
            return ctx.enter_context(nc.sbuf_tensor(f"p_{name}", shape, dt))

        def psum(name):
            return ctx.enter_context(nc.psum_tensor(f"p_{name}", [P, CH], F32))

        def sem(name):
            return ctx.enter_context(nc.semaphore(f"p_{name}"))

        small = [sb(f"small{i}", [P, NT]) for i in range(3)]
        an = [sb(f"an{i}", [P, CB, D]) for i in range(2)]
        anT = [sb(f"anT{i}", [P, CH]) for i in range(2)]
        rot = [[sb(f"rot{i}{k}", [P, CH]) for k in range(2)] for i in range(2)]
        tmp = [[sb(f"tmp{i}{k}", [P, CH]) for k in range(2)] for i in range(2)]
        rest = [[sb(f"rest{i}{k}", [P, CH]) for k in range(2)] for i in range(2)]
        part = [[[sb(f"part{i}{k}{m}", [P, CH], BF16) for m in range(KINDS)] for k in range(2)] for i in range(2)]
        psA, psV = psum("psA"), psum("psV")
        psP = [[psum(f"psP{i}{k}") for k in range(2)] for i in range(2)]
        stat_done, chain, square_ready, root_ready, normed, turned, turned_copied, v_done, v_copied = (
            sem(k) for k in ("stat_done", "chain", "square_ready", "root_ready", "normed", "turned",
                             "turned_copied", "v_done", "v_copied"))
        proj_done, rotated, summed, hi_done, rest_done, mid_done, lo_done = (
            [sem(f"{k}{i}") for i in range(2)] for k in (
                "proj_done", "rotated", "summed", "hi_done", "rest_done", "mid_done", "lo_done"))
        split_stored = [[sem(f"split_stored{i}{k}") for k in range(2)] for i in range(2)]
        block = ctx.enter_context(nc.Block())

        @block.vector
        def _(dve):
            link = Chain(dve, chain)
            token_stats(nc, dve, n, stat_done, link)
            rsqrt(nc, dve, link, n.rstd, n.mv[:, :, 1], *small, square_ready, root_ready, 1)

            def normalise(g, k):
                wait(dve, turned, g - 1)
                for j in range(CB):
                    last = nc.vector.tensor_scalar(an[k][:, j, :], n.tok[:, ds(g * CB + j, 1), :],
                                                   n.mv[:, ds(g * CB + j, 1), 0], n.rstd[:, ds(g * CB + j, 1)],
                                                   ALU.subtract, ALU.mult)
                last.then_inc(normed, 1)

            def rotate(g, k):
                for i in range(2):
                    dve.wait_ge(proj_done[i], g + 1)
                    wait(dve, lo_done[i], g - 1)
                    nc.vector.tensor_tensor(rot[i][k][:, :], psP[i][0][:, :], n.c("cos")[:, k * CH:(k + 1) * CH],
                                            ALU.mult)
                    nc.vector.tensor_tensor(tmp[i][k][:, :], psP[i][1][:, :], n.c("sin")[:, k * CH:(k + 1) * CH],
                                            ALU.mult).then_inc(rotated[i], 1)

            def subtract_hi(g, k):
                for i in range(2):
                    dve.wait_ge(hi_done[i], g + 1)
                    nc.vector.tensor_tensor(rest[i][k][:, :], rot[i][k][:, :], part[i][k][0][:, :],
                                            ALU.subtract).then_inc(rest_done[i], 1)

            normalise(0, 0)
            normalise(1, 1)
            rotate(0, 0)
            normalise(2, 0)
            rotate(1, 1)
            subtract_hi(0, 0)
            normalise(3, 1)
            with steps(dve, 2, NC8 - 2, 2) as g:
                rotate(g, 0)
                subtract_hi(g - 1, 1)
                normalise(g + 2, 0)
                rotate(g + 1, 1)
                subtract_hi(g, 0)
                normalise(g + 3, 1)
            rotate(NC8 - 2, 0)
            subtract_hi(NC8 - 3, 1)
            rotate(NC8 - 1, 1)
            subtract_hi(NC8 - 2, 0)
            subtract_hi(NC8 - 1, 1)

        @block.tensor
        def _(pe):
            def turn(g, k):
                pe.wait_ge(normed, g + 1)
                wait(pe, turned_copied, g)
                for j in range(CB):
                    last = nc.tensor.transpose(psA[:, j * P:(j + 1) * P], an[k][:, j, :], n.c("ident"))
                last.then_inc(turned, 1)

            def products(g, k):
                pe.wait_ge(turned_copied, g + 1)
                for i in range(2):
                    wait(pe, rotated[i], g)
                    for m in range(2):
                        last = nc.tensor.matmul(psP[i][m][:, :], n.wproj[:, 2 * i + m, :], anT[k][:, :],
                                                start=True, stop=True)
                    last.then_inc(proj_done[i], 1)
                wait(pe, v_copied, g)
                for j in range(CB):
                    last = nc.tensor.matmul(psV[:, j * P:(j + 1) * P], anT[k][:, j * P:(j + 1) * P],
                                            n.wproj[:, 4, :], start=True, stop=True)
                last.then_inc(v_done, 1)

            turn(0, 0)
            turn(1, 1)
            products(0, 0)
            turn(2, 0)
            products(1, 1)
            with steps(pe, 2, NC8 - 2, 2) as g:
                turn(g + 1, 1)
                products(g, 0)
                turn(g + 2, 0)
                products(g + 1, 1)
            turn(NC8 - 1, 1)
            products(NC8 - 2, 0)
            products(NC8 - 1, 1)

        @block.scalar
        def _(act):
            root_of(nc, act, small[1], small[0], square_ready, root_ready, 1)

            def copy_turned(g, k):
                act.wait_ge(turned, g + 1)
                wait(act, v_done, g - 1)
                nc.scalar.activation(anT[k][:, :], psA[:, :], ACT.Copy).then_inc(turned_copied, 1)

            def values_and_hi(g, k):
                act.wait_ge(v_done, g + 1)
                nc.scalar.activation(n.vals[:, ds((g - k) * 2, QB), k * CB:(k + 1) * CB, :],
                                     psV[:, :].rearrange("p (j q r) -> p q j r", j=CB, q=QB),
                                     ACT.Copy).then_inc(v_copied, 1)
                for i in range(2):
                    act.wait_ge(summed[i], g + 1)
                    wait(act, split_stored[i][k], 16 * KINDS // 2 * (g - k))
                    nc.scalar.activation(part[i][k][0][:, :], rot[i][k][:, :], ACT.Copy).then_inc(hi_done[i], 1)

            def mid(g, k):
                for i in range(2):
                    act.wait_ge(rest_done[i], g + 1)
                    nc.scalar.activation(part[i][k][1][:, :], rest[i][k][:, :], ACT.Copy).then_inc(mid_done[i], 1)

            copy_turned(0, 0)
            copy_turned(1, 1)
            values_and_hi(0, 0)
            copy_turned(2, 0)
            values_and_hi(1, 1)
            mid(0, 0)
            with steps(act, 2, NC8 - 2, 2) as g:
                copy_turned(g + 1, 1)
                values_and_hi(g, 0)
                mid(g - 1, 1)
                copy_turned(g + 2, 0)
                values_and_hi(g + 1, 1)
                mid(g, 0)
            copy_turned(NC8 - 1, 1)
            values_and_hi(NC8 - 2, 0)
            mid(NC8 - 3, 1)
            values_and_hi(NC8 - 1, 1)
            mid(NC8 - 2, 0)
            mid(NC8 - 1, 1)

        @block.gpsimd
        def _(pool):
            def add_pairs(g, k):
                for i in range(2):
                    pool.wait_ge(rotated[i], g + 1)
                    nc.gpsimd.tensor_tensor(rot[i][k][:, :], rot[i][k][:, :], tmp[i][k][:, :],
                                            ALU.add).then_inc(summed[i], 1)

            def subtract_mid(g, k):
                for i in range(2):
                    pool.wait_ge(mid_done[i], g + 1)
                    nc.gpsimd.tensor_tensor(part[i][k][2][:, :], rest[i][k][:, :], part[i][k][1][:, :],
                                            ALU.subtract).then_inc(lo_done[i], 1)

            add_pairs(0, 0)
            add_pairs(1, 1)
            with steps(pool, 2, NC8, 2) as g:
                for k in range(2):
                    subtract_mid(g - 2 + k, k)
                    add_pairs(g + k, k)
            subtract_mid(NC8 - 2, 0)
            subtract_mid(NC8 - 1, 1)

        @block.sync
        def _(sp):
            with steps(sp, 0, NC8, 2) as g:
                for k in range(2):
                    for i in range(2):
                        sp.wait_ge(lo_done[i], g + k + 1)
                        for m in range(KINDS):
                            rows = slice(m * DK, (m + 1) * DK)
                            if i == 0:
                                there = n.q_dram[rows, k, ds(g * (H // 2), H), :]
                            else:
                                there = n.k_dram[rows, ds(g * (H // 2), H), k * CH:(k + 1) * CH]
                            sp.dma_start(there.rearrange("d h t -> h d t"),
                                         part[i][k][m][:, :]).then_inc(split_stored[i][k], 16)
            for i in range(2):
                for k in range(2):
                    sp.wait_ge(split_stored[i][k], 16 * KINDS * NC8 // 2)


def attention(nc, n):
    units = []
    for ch in range(NCH):
        for j in range((ch + 1) * CB):
            q0 = max(j * P, ch * CH)
            units.append((ch, j, q0, (ch + 1) * CH - q0))
    UN = len(units)
    SC = UN * QH
    diagonal = [u for u, (ch, j, q0, w) in enumerate(units) if j * P == q0]
    half_start = [0, CB]
    half_end = [CB, UN]
    tiles = [((h, h + 1), i) for i in range(CB) for h in range(0, QH, 2)]
    HALF_TILES = len(tiles)
    tiles += [((h,), i) for i in range(CB, TB) for h in range(QH)]
    MT = len(tiles)

    tile_cost = [len(heads) * (i + 1) * P + 120 for heads, i in tiles]
    tile_total = sum(tile_cost)
    att_total = sum(2 * w * QH for _, _, _, w in units)

    def plan(first, last):
        found, att, tile = [], 0, 0

        def spread():
            nonlocal tile
            while not last and tile < MT and sum(tile_cost[:tile + 1]) * att_total <= att * tile_total + AHEAD:
                found.append(("tile", tile, 0))
                tile += 1

        for u in range(UN):
            w = units[u][3]
            for h in range(QH):
                found.append(("score", u, h))
                att += w
                if h == 1:
                    if u >= LAG:
                        found.append(("weigh", u - LAG, 0))
                        att += QH * units[u - LAG][3]
                    elif not first:
                        found.append(("weigh", u - LAG, 1))
                        att += QH * units[u - LAG + UN][3]
                spread()
            for at, what, arg, there in EXTRAS:
                if at == u and (there or not (first if arg == 1 and what == "turn_out" else last)):
                    found.append((what, arg, 0))
        att = att_total * 2
        spread()
        return found

    def uses(first, last):
        return [(0, what, arg) for what, arg, _ in plan(first, last) if what in ("tile", "turn_max", "turn_out")]

    LAG = 2
    AHEAD = tile_total * tile_cost[0] // 2
    EXTRAS = [(1, "turn_max", 1, True), (3, "turn_out", 1, False), (7, "turn_out", 0, True),
              (8, "turn_max", 0, False)]
    before_loop = [(0, "tile", t) for t in range(MT // 2)] + [(0, "turn_max", 0)]
    before_loop += [(0, "tile", t) for t in range(MT // 2, MT)]
    USES = len(uses(False, False))

    def base(s, first):
        return len(before_loop) if first else len(before_loop) + len(uses(True, False)) + (s - 1) * USES

    PARITY = base(1, False) % 2
    assert USES % 2 == 0

    def q_col(h, q):
        return (q // CH * QH + h) * CH + q % CH

    with ExitStack() as ctx:
        def sb(name, shape, dt=F32):
            return ctx.enter_context(nc.sbuf_tensor(f"a_{name}", shape, dt))

        def psum(name, width):
            return ctx.enter_context(nc.psum_tensor(f"a_{name}", [P, width], F32))

        def sem(name):
            return ctx.enter_context(nc.semaphore(f"a_{name}"))

        qs = [sb(f"qs{i}", [PR + MR, QH * S], BF16) for i in range(RING)]
        ks, vs = n.ks, n.vs
        MP = KINDS * QH * CB
        prob = sb("prob", [P, RING, QH, CH])
        rowmax = sb("rowmax", [P, QH, TB])
        maxparts = sb("maxparts", [P, P], BF16)
        maxrest = [sb(f"maxrest{i}", [P, QH, CB]) for i in range(2)]
        maxT = [sb(f"maxT{i}", [MP, P], BF16) for i in range(2)]
        zeros = sb("zeros", [P, QH, CB])
        gate = sb("gate", [1, UN])
        outT = sb("outT", [P, CH])
        recip = [sb(f"recip{i}", [P, CB, QH]) for i in range(NCH)]
        psST = [psum(f"psST{i}", CH) for i in range(3)]
        psS = [psum(f"psS{i}", 2 * CH) for i in range(2)]
        psO = psum("psO", CH)
        maxpart = maxparts[:, 0:MP].rearrange("p (k h i) -> p k h i", k=KINDS, h=QH)
        QB = H // QH

        (cleared, v_ready, scored, use_done, use_read, exp_done, masked, pv_done, out_copied, split_done,
         maxT_ready, split_chain, out_read) = (sem(k) for k in (
             "cleared", "v_ready", "scored", "use_done", "use_read", "exp_done", "masked", "pv_done",
             "out_copied", "split_done", "maxT_ready", "split_chain", "out_read"))
        stack_loaded = [sem(f"stack_loaded{i}") for i in range(RING)]
        max_loaded = [sem(f"max_loaded{i}") for i in range(2)]
        STACK_DMAS = 1 + KINDS * NCH
        block = ctx.enter_context(nc.Block())

        def run(eng, stage):
            stage(0, 0, 0, True, False)
            with eng.Fori(0, (NST - 4) // RING) as i:
                for k in range(1, RING + 1):
                    stage(i * RING + k, k % RING, i + k // RING, False, False)
            for s in range(NST - RING, NST):
                stage(s, s % RING, s // RING, False, s == NST - 1)

        @block.sync
        def _(sp):
            def load(s, r):
                wait(sp, scored, (s - RING + 1) * SC)
                sp.dma_start(ks[r][0:PR, :], n.k_dram[:, ds(s * QH, QH), :].rearrange("d h t -> d (h t)")
                             .unsqueeze(0).to_broadcast([KINDS, KINDS * DK, QH * S])).then_inc(stack_loaded[r], 16)
                for ch in range(NCH):
                    for kind in range(KINDS):
                        sp.dma_start(qs[r][kind * KINDS * DK:(kind + 1) * KINDS * DK,
                                           ch * QH * CH:(ch + 1) * QH * CH],
                                     n.q_dram[kind * DK:(kind + 1) * DK, ch, ds(s * QH, QH), :]
                                     .rearrange("d h t -> d (h t)").unsqueeze(0)
                                     .to_broadcast([KINDS, DK, QH * CH])).then_inc(stack_loaded[r], 16)

            def load_max(s, r, half):
                sp.wait_ge(maxT_ready, 2 * s + half + 1)
                sp.dma_start(qs[r][PR:PR + MR, half * QH * CH:(half + 1) * QH * CH],
                             maxT[half][:, :]).then_inc(max_loaded[half], 16)

            def stage(s, r, turn, first, last):
                if not first and not last and not (isinstance(s, int) and s + 2 >= NST):
                    load(s + 2, (r + 2) % RING)
                load_max(s, r, 1)
                if not last:
                    load_max(s + 1, (r + 1) % RING, 0)

            load(0, 0)
            load(1, 1)
            load_max(0, 0, 0)
            load(2, 2)
            run(sp, stage)

        @block.tensor
        def _(pe):
            def use(index):
                wait(pe, use_read, index - 1)

            def tile(r, turn, t, index, ps):
                heads, i = tiles[t]
                if t == 0:
                    pe.wait_ge(stack_loaded[r], (turn + 1) * 16 * STACK_DMAS)
                use(index)
                width = (i + 1) * P
                for a, h in enumerate(heads):
                    lhs = qs[r][0:PR, q_col(h, i * P):q_col(h, i * P) + P]
                    for c0 in range(0, width, CH):
                        w = min(CH, width - c0)
                        nc.tensor.matmul(ps[:, a * CH + c0:a * CH + c0 + w], lhs,
                                         ks[r][0:PR, h * S + c0:h * S + c0 + w], start=True, stop=c0 + w < width)
                    last = nc.tensor.matmul(ps[:, a * CH + i * P:a * CH + width], n.identb[:, :], n.maskb[:, :],
                                            start=False, stop=True)
                last.then_inc(use_done, 1)

            def turn_max(s, half, index, ps):
                use(index)
                pe.wait_ge(split_done, 2 * s + half + 1)
                nc.tensor.transpose(ps[:, 0:P // 2].bitcast(BF16), maxparts[:, :], n.identb[:, :]).then_inc(use_done, 1)

            def turn_out(s, ch, index, ps):
                use(index)
                pe.wait_ge(out_copied, 2 * s + ch + 1)
                for b in range(CB):
                    last = nc.tensor.transpose(ps[:, b * P:(b + 1) * P], outT[:, b * P:(b + 1) * P], n.c("ident"))
                last.then_inc(use_done, 1)

            def score(s, r, u, h):
                ch, j, q0, w = units[u]
                if u in half_start and h == 0:
                    half = half_start.index(u)
                    pe.wait_ge(max_loaded[half], (s + 1) * 16)
                wait(pe, exp_done, s * SC + u * QH + h - 2)
                nc.tensor.matmul(psST[(u * QH + h) % 3][:, 0:w], ks[r][:, h * S + j * P:h * S + (j + 1) * P],
                                 qs[r][:, q_col(h, q0):q_col(h, q0) + w], start=True, stop=True).then_inc(scored, 1)

            def weigh(s, r, u):
                ch, j, q0, w = units[u]
                pe.wait_ge(exp_done, s * SC + (u + 1) * QH)
                if u in diagonal:
                    pe.wait_ge(masked, s * len(diagonal) + diagonal.index(u) + 1)
                if u in half_start:
                    pe.wait_ge(v_ready, s + 1)
                    wait(pe, out_copied, 2 * s + half_start.index(u))
                c0 = q0 - ch * CH
                for h in range(QH):
                    last = nc.tensor.matmul(psO[32 * h:32 * h + 32, c0:c0 + w], vs[r][:, j, h, :],
                                            prob[:, u % RING, h, 0:w], start=(j == 0),
                                            stop=(u + 1 in half_end))
                last.then_inc(pv_done, 1)

            def stage(s, r, turn, first, last):
                b, parity = base(s, first), base(0, True) % 2 if first else PARITY
                k = 0
                for what, arg, arg2 in plan(first, last):
                    if what == "score":
                        score(s, r, arg, arg2)
                        continue
                    if what == "weigh":
                        if arg2:
                            weigh(s - 1, (r - 1) % RING, arg + UN)
                        else:
                            weigh(s, r, arg)
                        continue
                    ps = psS[(parity + k) % 2]
                    if what == "tile":
                        tile((r + 1) % RING, turn + (r + 1) // RING, arg, b + k, ps)
                    elif what == "turn_max":
                        turn_max(s if arg else s + 1, arg, b + k, ps)
                    else:
                        turn_out(s - 1 if arg else s, arg, b + k, ps)
                    k += 1

            for k, (_, what, arg) in enumerate(before_loop):
                if what == "tile":
                    tile(0, 0, arg, k, psS[k % 2])
                else:
                    turn_max(0, arg, k, psS[k % 2])
            run(pe, stage)
            weigh(NST - 1, (NST - 1) % RING, UN - 2)
            weigh(NST - 1, (NST - 1) % RING, UN - 1)
            end = base(NST - 1, False) + len(uses(False, True))
            turn_out(NST - 1, 1, end, psS[end % 2])

        @block.scalar
        def _(act):
            def exps(s, u):
                ch, j, q0, w = units[u]
                wait(act, pv_done, s * UN + u - 2)
                for h in range(QH):
                    act.wait_ge(scored, s * SC + u * QH + h + 1)
                    nc.scalar.activation(prob[:, u % RING, h, 0:w], psST[(u * QH + h) % 3][:, 0:w], ACT.Exp,
                                         scale=SCALE).then_inc(exp_done, 1)

            def copy_out(s, ch):
                act.wait_ge(pv_done, s * UN + half_end[ch])
                wait(act, out_read, 2 * s + ch)
                nc.scalar.activation(outT[:, :], psO[:, :], ACT.Copy).then_inc(out_copied, 1)

            def stage(s, r, turn, first, last):
                for u in range(UN):
                    if u == 1 and not first:
                        copy_out(s - 1, 1)
                    if u == half_end[0] + 1:
                        copy_out(s, 0)
                    exps(s, u)

            run(act, stage)
            copy_out(NST - 1, 1)

        @block.vector
        def _(dve):
            nc.vector.memset(maxparts[:, :], 0.0)
            nc.vector.memset(zeros[:, :, :], 0.0).then_inc(cleared, 1)

            def reduce(s, t, index, ps):
                heads, i = tiles[t]
                if t in (0, HALF_TILES):
                    wait(dve, split_done, 2 * s - 1 + (t > 0))
                dve.wait_ge(use_done, index + 1)
                width = (i + 1) * P
                if len(heads) == 2:
                    src = ps[:, :].rearrange("p (a c) -> p a c", a=2)[:, :, 0:width]
                    nc.vector.reduce_max(rowmax[:, heads[0]:heads[0] + 2, i], src, AX.X).then_inc(use_read, 1)
                else:
                    nc.vector.reduce_max(rowmax[:, heads[0]:heads[0] + 1, i], ps[:, 0:width],
                                         AX.X).then_inc(use_read, 1)

            def copy_max(s, half, index, ps):
                dve.wait_ge(use_done, index + 1)
                wait(dve, max_loaded[half], s * 16)
                nc.vector.tensor_copy(maxT[half][:, :],
                                      ps[0:MP, 0:P // 2].bitcast(BF16)).then_inc(use_read, 1)
                dve.wait_ge(use_read, index + 1)
                dve.sem_inc(maxT_ready, 1)

            def normalise(s, ch, index, ps):
                dve.wait_ge(use_done, index + 1)
                src = ps[:, 0:CH].rearrange("p (b h c) -> p b h c", b=CB, h=QH)
                nc.vector.reciprocal(recip[ch][:, :, :], src[:, :, :, DK]).then_inc(out_read, 1)
                dve.wait_ge(out_read, 2 * s + ch + 1)
                nc.vector.tensor_tensor(
                    n.shared[:, ds((s // QB) * TB + ch * CB, CB), ds((s % QB) * RW, RW)]
                    .rearrange("p j (h d) -> p j h d", h=QH),
                    src[:, :, :, 0:DK], recip[ch][:, :, :].unsqueeze(3).to_broadcast([P, CB, QH, DK]),
                    ALU.mult).then_inc(use_read, 1)

            def do(s, what, arg, index, ps):
                if what == "tile":
                    reduce(s + 1, arg, index, ps)
                elif what == "turn_max":
                    copy_max(s if arg else s + 1, arg, index, ps)
                else:
                    normalise(s - 1 if arg else s, arg, index, ps)

            def stage(s, r, turn, first, last):
                b, parity = base(s, first), base(0, True) % 2 if first else PARITY
                for k, (_, what, arg) in enumerate(uses(first, last)):
                    do(s, what, arg, b + k, psS[(parity + k) % 2])

            for k, (_, what, arg) in enumerate(before_loop):
                do(-1, what, arg, k, psS[k % 2])
            run(dve, stage)
            end = base(NST - 1, False) + len(uses(False, True))
            normalise(NST - 1, 1, end, psS[end % 2])

        @block.gpsimd
        def _(pool):
            half_ready = {}
            for what, found in (("first", uses(True, False)), ("middle", uses(False, False))):
                for half, t in ((0, HALF_TILES - 1), (1, MT - 1)):
                    half_ready[what, half] = [k for k, (_, w, a) in enumerate(found) if (w, a) == ("tile", t)][0] + 1
            def split(s, half, count, order):
                pool.wait_ge(use_read, count)
                wait(pool, maxT_ready, 2 * s + half)
                src = rowmax[:, :, half * CB:(half + 1) * CB]
                done = order * 4

                def link(ins, k):
                    ins.then_inc(split_chain, 1)
                    pool.wait_ge(split_chain, done + k)

                zero = zeros[:, :, :]
                link(nc.gpsimd.tensor_tensor(maxpart[:, 0, :, :], zero, src, ALU.subtract), 1)
                link(nc.gpsimd.tensor_tensor(maxrest[0][:, :, :], src, maxpart[:, 0, :, :], ALU.add), 2)
                link(nc.gpsimd.tensor_tensor(maxpart[:, 1, :, :], zero, maxrest[0][:, :, :], ALU.subtract), 3)
                link(nc.gpsimd.tensor_tensor(maxrest[1][:, :, :], maxrest[0][:, :, :], maxpart[:, 1, :, :],
                                             ALU.add), 4)
                nc.gpsimd.tensor_tensor(maxpart[:, 2, :, :], zero, maxrest[1][:, :, :],
                                        ALU.subtract).then_inc(split_done, 1)

            def values(s, r):
                wait(pool, pv_done, (s - RING + 1) * UN + 1)
                nc.gpsimd.tensor_copy(vs[r][:, :, :, 0:DK],
                                      n.vals[:, ds(s, 1), :, :].rearrange("p s j (h d) -> p (s j) h d", h=QH)
                                      ).then_inc(v_ready, 1)

            def mask(s, u):
                pool.wait_ge(exp_done, s * SC + (u + 1) * QH)
                part = prob[:, u % RING, :, 0:P]
                nc.gpsimd.tensor_tensor(gate[:, u:u + 1], zeros[0:1, 0, 0:1], zeros[0:1, 0, 1:2], ALU.add)
                nc.gpsimd.affine_select(out=part, in_=part, compare_op=ALU.is_ge, fill=0.0, base=0,
                                        pattern=[[0, QH], [1, P]], channel_multiplier=-1).then_inc(masked, 1)

            def stage(s, r, turn, first, last):
                for u in diagonal:
                    if u == half_end[0] + CB:
                        if not last:
                            split(s + 1, 0, base(s, first) + half_ready["first" if first else "middle", 0],
                                  2 * s + 2)
                            values(s + 1, (r + 1) % RING)
                    mask(s, u)
                if not last:
                    split(s + 1, 1, base(s, first) + half_ready["first" if first else "middle", 1], 2 * s + 3)

            pool.wait_ge(cleared, 1)
            nc.gpsimd.tensor_copy(vs[0][:, :, :, 0:DK],
                                  n.vals[:, 0, :, :].rearrange("p j (h d) -> p j h d", h=QH)).then_inc(v_ready, 1)
            split(0, 0, HALF_TILES, 0)
            split(0, 1, len(before_loop), 1)
            run(pool, stage)


def output_projection(nc, n):
    QB = H // QH
    G = NT // CB
    with ExitStack() as ctx:
        oT = [ctx.enter_context(nc.sbuf_tensor(f"o_T{i}", [P, CH], F32)) for i in range(2)]
        psT = [ctx.enter_context(nc.psum_tensor(f"o_psT{i}", [P, CH], F32)) for i in range(2)]
        psY = [ctx.enter_context(nc.psum_tensor(f"o_psY{i}", [P, CH], F32)) for i in range(2)]
        turned, turned_copied, projected, added = (ctx.enter_context(nc.semaphore(f"o_{k}")) for k in (
            "turned", "turned_copied", "projected", "added"))
        block = ctx.enter_context(nc.Block())

        @block.tensor
        def _(pe):
            def product(g):
                pe.wait_ge(turned_copied, g + 1)
                wait(pe, added, g - 1)
                for j in range(CB):
                    last = nc.tensor.matmul(psY[g % 2][:, j * P:(j + 1) * P], oT[g % 2][:, j * P:(j + 1) * P],
                                            n.wproj[:, 5, :], start=True, stop=True)
                last.then_inc(projected, 1)

            for g in range(G):
                wait(pe, turned_copied, g - 1)
                for j in range(CB):
                    last = nc.tensor.transpose(psT[g % 2][:, j * P:(j + 1) * P],
                                               n.shared[:, g * CB + j, :], n.c("ident"))
                last.then_inc(turned, 1)
                if g >= 1:
                    product(g - 1)
            product(G - 1)

        @block.scalar
        def _(act):
            for g in range(G):
                act.wait_ge(turned, g + 1)
                wait(act, projected, g - 1)
                nc.scalar.activation(oT[g % 2][:, :], psT[g % 2][:, :], ACT.Copy).then_inc(turned_copied, 1)

        @block.vector
        def _(dve):
            for g in range(G):
                dve.wait_ge(projected, g + 1)
                part = n.tok[:, g * CB:(g + 1) * CB, :]
                nc.vector.tensor_tensor(part, part, psY[g % 2][:, :].rearrange("p (j d) -> p j d", j=CB),
                                        ALU.add).then_inc(added, 1)


_OUT = (B, S, D)


def kernel(**inputs):
    import concourse.bacc as bacc
    from concourse.bass_utils import run_bass_kernel_spmd

    def arr(name):
        return np.ascontiguousarray(inputs[name])

    def swapped(w):
        return np.ascontiguousarray(w.reshape(D // 2, 2, D)[:, ::-1, :].reshape(D, D).T)

    wq, wk = arr("L0_attn_Wq"), arr("L0_attn_Wk")
    arrays = {
        "x": arr("L0_attn_x"), "WqT": np.ascontiguousarray(wq.T), "WqsT": swapped(wq),
        "WkT": np.ascontiguousarray(wk.T), "WksT": swapped(wk),
        "WvT": np.ascontiguousarray(arr("L0_attn_Wv").T), "WoT": np.ascontiguousarray(arr("L0_attn_Wo").T),
        "Wr": arr("L0_ffn_Wr"), "br": arr("L0_ffn_br"), "ln_g": arr("L0_ffn_ln_g"), "ln_b": arr("L0_ffn_ln_b"),
        "W1": arr("L0_ffn_W1"), "b1": arr("L0_ffn_b1"), "W2": arr("L0_ffn_W2"), "b2": arr("L0_ffn_b2"),
        "const": constants(),
    }
    nc = bacc.Bacc("TRN2", target_bir_lowering=False, num_devices=1)
    args = {k: nc.dram_tensor(f"in_{k}", a.shape, mybir.dt.from_np(a.dtype), kind="ExternalInput").ap()
            for k, a in arrays.items()}
    out = nc.dram_tensor("out_x", _OUT, F32, kind="ExternalOutput").ap()
    build(nc, out=out, **args)
    result = run_bass_kernel_spmd(nc, [{f"in_{k}": a for k, a in arrays.items()}], core_ids=[0])
    return result.results[0]["out_x"]
```

```python
from contextlib import ExitStack, contextmanager

import numpy as np

import concourse.bass as bass
from concourse import mybir

F32 = mybir.dt.float32
BF16 = mybir.dt.bfloat16
U32 = mybir.dt.uint32
I32 = mybir.dt.int32
ALU = mybir.AluOpType
ACT = mybir.ActivationFunctionType
AX = mybir.AxisListType

B, S, D = 4, 1024, 128
H, DK = 16, 8
E, F = 8, 512
P = 128
NT = B * S // P
TB = S // P
FB = F // P
NS = NT + E
EPS = 1e-5
SCALE = DK ** -0.5
NEG = -1e30
QH = 4
NST = B * H // QH
RW = QH * DK
KINDS = 3
PR = KINDS * KINDS * DK
MR = KINDS
CH = 512
NCH = S // CH
CB = CH // P
TW = 2 * D + 2
HALF_GATE, NUMBER = 2 * D, 2 * D + 1
W1W, W2W = F + FB, FB * D + D
CLEAR = 4
LR = 8
RING = 3

CONST = {}
_at = 0
for _name, _width in (("ident", P), ("before", P), ("mask", P), ("ramp", E), ("full", NT),
                      ("tri", E * E), ("tile", NS), ("number", NT), ("pad", 1), ("cos", S), ("sin", S)):
    CONST[_name] = (_at, _at + _width)
    _at += _width
CONST_W = _at


def constants():
    t = np.zeros((P, CONST_W), np.float32)

    def put(name, a):
        t[:, CONST[name][0]:CONST[name][1]] = a

    i = np.arange(P)
    put("ident", np.eye(P))
    put("before", i[:, None] < i[None, :])
    put("mask", np.where(i[None, :] <= i[:, None], 0.0, NEG))
    put("ramp", np.arange(E, 0, -1))
    put("full", P * np.arange(NT))
    put("tri", (np.arange(E)[None, :] < np.arange(E)[:, None]).reshape(1, -1))
    put("tile", np.arange(NS))
    put("number", P * np.arange(NT)[None, :] + i[:, None])
    put("pad", B * S + i[:, None])
    half = DK // 2
    freq = np.float32(10000.0) ** (-np.arange(0, half, dtype=np.float32) * np.float32(2.0) / np.float32(DK))
    angle = np.arange(S, dtype=np.float32)[None, :] * freq[:, None].astype(np.float32)
    row = (i % DK) // 2
    put("cos", np.cos(angle)[row])
    put("sin", np.sin(angle)[row] * np.where(i % 2 == 0, -1.0, 1.0)[:, None])
    return t


def ds(start, size):
    return bass.ds(start, size)


@contextmanager
def steps(eng, start, end, step):
    with eng.Fori(start // step, end // step) as i:
        yield i * step


def wait(eng, sem, value):
    if isinstance(value, int) and value <= 0:
        return
    eng.wait_ge(sem, value)


class Chain:

    def __init__(self, eng, sem):
        self.eng, self.sem, self.n = eng, sem, 0

    def __call__(self, ins):
        self.n += 1
        ins.then_inc(self.sem, 1)
        self.eng.wait_ge(self.sem, self.n)


class Kept:
    pass


def build(nc, x, Wp, Wr, br, ln, Wb1, W2, b2, const, out):
    ctx = ExitStack()
    with ctx:
        def sb(name, shape, dt=F32):
            return ctx.enter_context(nc.sbuf_tensor(name, shape, dt))

        n = Kept()
        n.x, n.Wp, n.Wr, n.br, n.ln, n.Wb1, n.W2, n.b2, n.const = x, Wp, Wr, br, ln, Wb1, W2, b2, const
        n.tok = sb("tok", [P, NT, TW])
        n.cst = sb("cst", [P, CONST_W])
        n.identb = sb("identb", [P, P], BF16)
        n.beforeb = sb("beforeb", [P, P], BF16)
        n.maskb = sb("maskb", [P, P], BF16)
        n.onesb = sb("onesb", [P, P], BF16)
        n.wproj = sb("wproj", [P, 6, D])
        n.wr = sb("wr", [P, E])
        n.gb = sb("gb", [P, 2])
        n.brb = sb("brb", [P, E])
        n.w1 = sb("w1", [P, E, W1W])
        n.w2 = sb("w2", [P, E, W2W])
        n.mean = sb("mean", [P, NT])
        n.blank = sb("blank", [P, CLEAR, TW])
        n.stats = sb("stats", [P, NT, 6])
        n.var = sb("var", [P, NT])
        n.rstd = sb("rstd", [P, NT])
        n.shared = n.tok[:, :, D:2 * D]
        n.vals = sb("vals", [P, NST, TB, RW])

        n.ks = [sb(f"ks{i}", [PR + MR, QH * S], BF16) for i in range(RING)]
        n.vs = [sb(f"vs{i}", [P, TB, QH, 32]) for i in range(RING)]

        def c(name, rows=P):
            return n.cst[0:rows, CONST[name][0]:CONST[name][1]]

        n.q_dram = nc.dram_tensor("q_split", (KINDS * DK, NCH, B * H, CH), BF16, kind="Internal").ap()
        n.k_dram = nc.dram_tensor("k_split", (KINDS * DK, B * H, S), BF16, kind="Internal").ap()
        n.sort_dram = [nc.dram_tensor(f"sorted{r}", (NS * P, TW), F32, kind="Internal").ap() for r in range(2)]
        n.x_dram = nc.dram_tensor("x_after_first", (B * S, D), F32, kind="Internal").ap()

        def sem(name):
            return ctx.enter_context(nc.semaphore(name))

        n.x_loaded = [sem(f"x_loaded{b}") for b in range(B)]
        n.table_loaded, n.router_loaded, n.weights_loaded = sem("table_loaded"), sem("router_loaded"), sem("weights_loaded")
        n.blank_ready, n.numbered = sem("blank_ready"), sem("numbered")
        n.blanks_written = [sem(f"blanks_written{r}") for r in range(2)]
        n.ring_init = sem("ring_init")
        n.c = c
        setup(nc, n)
        ffn(nc, n, 0, n.x_dram)
        project(nc, n)
        attention(nc, n)
        output_projection(nc, n)
        ffn(nc, n, 1, out.rearrange("b s d -> (b s) d"))


HEAD_W = CONST["cos"][0]


def setup(nc, n):
    with ExitStack() as ctx:
        block = ctx.enter_context(nc.Block())

        def load_x(eng, b):
            eng.dma_start(n.tok[:, b * TB:(b + 1) * TB, 0:D],
                          n.x[b].rearrange("(n p) d -> p n d", p=P)).then_inc(n.x_loaded[b], 16)

        @block.sync
        def _(sp):
            load_x(sp, 0)
            load_x(sp, 2)
            sp.dma_start(n.cst[:, 0:HEAD_W], n.const[:, 0:HEAD_W]).then_inc(n.table_loaded, 16)
            sp.dma_start(n.w1[:, :, :], n.Wb1).then_inc(n.weights_loaded, 16)
            sp.dma_start(n.cst[:, HEAD_W:], n.const[:, HEAD_W:]).then_inc(n.weights_loaded, 16)
            sp.dma_start(n.wproj[:, :, :], n.Wp).then_inc(n.weights_loaded, 16)

        @block.scalar
        def _(act):
            load_x(act, 1)
            load_x(act, 3)
            act.dma_start(n.wr[:, :], n.Wr).then_inc(n.router_loaded, 16)
            act.dma_start(n.gb[:, :], n.ln).then_inc(n.router_loaded, 16)
            act.dma_start(n.brb[:, :], n.br.partition_broadcast(P)).then_inc(n.router_loaded, 16)
            act.dma_start(n.w2[:, :, FB * D:], n.b2.partition_broadcast(P)).then_inc(n.weights_loaded, 16)
            act.dma_start(n.w2[:, :, 0:FB * D], n.W2).then_inc(n.weights_loaded, 16)

        @block.vector
        def _(dve):
            nc.vector.memset(n.onesb[:, :], 1.0)
            nc.vector.memset(n.blank[:, :, :], 0.0)


LOADS = 5


def first_block_pool(nc, pool, n):
    pool.wait_ge(n.table_loaded, 16)
    nc.gpsimd.tensor_copy(n.tok[:, :, NUMBER].bitcast(U32), n.c("number")).then_inc(n.numbered, 1)
    nc.gpsimd.tensor_copy(n.blank[:, :, NUMBER].bitcast(U32),
                          n.c("pad").to_broadcast([P, CLEAR])).then_inc(n.blank_ready, 1)
    link = Chain(pool, n.ring_init)
    link(nc.gpsimd.tensor_copy(n.maskb[:, :], n.c("mask")))
    for r in range(RING):
        link(nc.gpsimd.memset(n.ks[r][64:PR + MR, :], 1.0))
        link(nc.gpsimd.memset(n.vs[r][:, :, :, DK + 1:], 0.0))
        link(nc.gpsimd.memset(n.vs[r][:, :, :, DK:DK + 1], 1.0))


def write_blanks(sp, n):
    sp.wait_ge(n.blank_ready, 1)
    for r in range(2):
        for k in range(NS // CLEAR):
            sp.dma_start(n.sort_dram[r][k * CLEAR * P:(k + 1) * CLEAR * P, :].rearrange("(a p) d -> p a d", p=P),
                         n.blank[:, :, :]).then_inc(n.blanks_written[r], 16)
    sp.wait_ge(n.weights_loaded, 16 * LOADS)


def token_stats(nc, dve, n, stat_done, link, ready):
    for t in range(NT):
        if ready is not None and t % TB == 0:
            dve.wait_ge(ready[t // TB], 16)
        nc.vector.bn_stats(n.stats[:, t, :], n.tok[:, t, 0:D]).then_inc(stat_done, 1)
    dve.wait_ge(stat_done, NT)
    mean, var = n.mean[:, :], n.var[:, :]
    even, odd, sq_even, sq_odd = (n.stats[:, :, k] for k in (1, 4, 2, 5))
    link(nc.vector.tensor_tensor(mean, even, odd, ALU.add))
    link(nc.vector.tensor_scalar(mean, mean, 0.5, None, ALU.mult))
    link(nc.vector.tensor_tensor(var, sq_even, sq_odd, ALU.add))
    link(nc.vector.tensor_tensor(even, even, odd, ALU.subtract))
    link(nc.vector.scalar_tensor_tensor(even, even, 0.25, even, ALU.mult, ALU.mult))
    link(nc.vector.scalar_tensor_tensor(var, var, 1.0 / D, even, ALU.mult, ALU.add))


def rsqrt(nc, dve, link, out, var, shifted, root, corr, square_ready, root_ready, turn):
    nc.vector.tensor_scalar(shifted[:, :], var, EPS, None, ALU.add).then_inc(square_ready, 1)
    dve.wait_ge(root_ready, turn)
    link(nc.vector.reciprocal(out[:, :], root[:, :]))
    link(nc.vector.tensor_tensor(corr[:, :], out[:, :], out[:, :], ALU.mult))
    link(nc.vector.tensor_tensor(corr[:, :], corr[:, :], shifted[:, :], ALU.mult))
    link(nc.vector.tensor_scalar(corr[:, :], corr[:, :], -0.5, 1.5, ALU.mult, ALU.add))
    link(nc.vector.tensor_tensor(out[:, :], out[:, :], corr[:, :], ALU.mult))


def root_of(nc, act, root, shifted, square_ready, root_ready, turn):
    act.wait_ge(square_ready, turn)
    nc.scalar.activation(root[:, :], shifted[:, :], ACT.Sqrt).then_inc(root_ready, 1)


def ffn(nc, n, r, target):
    NCHK = NT // 4
    outer = ExitStack()
    with outer:
        def sb(name, shape, dt=F32):
            return outer.enter_context(nc.sbuf_tensor(f"f{r}_{name}", shape, dt))

        pos = sb("pos", [P, NT], U32)
        tile_expert = sb("tile_expert", [1, NS], I32)
        small = [sb(f"small{i}", [P, NT]) for i in range(6)]
        lg = [sb(f"lg{i}", [P, NT, E]) for i in range(3)]
        onehot = sb("onehot", [P, NT, E], BF16)
        cnt = sb("cnt", [P, E])
        ntile = sb("ntile", [P, E])
        first = sb("first", [P, E])
        xT = [sb(f"xT{i}", [P, 4 * P]) for i in range(2)]
        te = sb("te", [1, NS, E])
        tef = sb("tef", [1, NS])

        with ExitStack() as ctx:
            def sem(name):
                return ctx.enter_context(nc.semaphore(f"f{r}_{name}"))

            psT = [ctx.enter_context(nc.psum_tensor(f"f{r}_psT{i}", [P, 512], F32)) for i in range(2)]
            psL = ctx.enter_context(nc.psum_tensor(f"f{r}_psL", [P, NT, E], F32))
            psR = ctx.enter_context(nc.psum_tensor(f"f{r}_psR", [P, NT, E], F32))
            psC = ctx.enter_context(nc.psum_tensor(f"f{r}_psC", [P, E], F32))
            stat_done, chain = sem("stat_done"), sem("chain")
            square_ready, root_ready = sem("square_ready"), sem("root_ready")
            normed, turned, turned_copied, logits_done = (sem("normed"), sem("turned"), sem("turned_copied"),
                                                          sem("logits_done"))
            shifted, exp_done, onehot_ready, ranks_done = (sem("shifted"), sem("exp_done"), sem("onehot_ready"),
                                                           sem("ranks_done"))
            pos_ready, scattered, tables_rounded = sem("pos_ready"), sem("scattered"), sem("tables_rounded")
            block = ctx.enter_context(nc.Block())

            @block.vector
            def _(dve):
                link = Chain(dve, chain)
                token_stats(nc, dve, n, stat_done, link, n.x_loaded if r == 0 else None)
                rstd_u, scale, inv_u, shift, root, corr = small
                rsqrt(nc, dve, link, n.rstd, n.var[:, :], shift, root, corr, square_ready, root_ready, 1)
                link(nc.vector.tensor_tensor(scale[:, :], n.rstd[:, :], n.rstd[:, :], ALU.mult))
                link(nc.vector.tensor_tensor(scale[:, :], scale[:, :], n.var[:, :], ALU.mult))
                rsqrt(nc, dve, link, rstd_u, scale[:, :], shift, root, corr, square_ready, root_ready, 2)
                link(nc.vector.tensor_tensor(inv_u[:, :], shift[:, :], rstd_u[:, :], ALU.mult))
                link(nc.vector.tensor_tensor(scale[:, :], n.rstd[:, :], rstd_u[:, :], ALU.mult))
                for t in range(NT):
                    nc.vector.tensor_scalar(n.shared[:, t, :], n.tok[:, t, 0:D], n.mean[:, t:t + 1],
                                            scale[:, t:t + 1],
                                            ALU.subtract, ALU.mult).then_inc(normed, 1)
                logit, other, rank = lg
                dve.wait_ge(logits_done, NT)
                dve.wait_ge(n.table_loaded, 16)
                dve.wait_ge(n.router_loaded, 16 * 3)
                link(nc.vector.tensor_tensor(logit[:, :, :], psL[:, :, :],
                                             inv_u[:, :].unsqueeze(2).to_broadcast([P, NT, E]), ALU.mult))
                link(nc.vector.tensor_tensor(logit[:, :, :], logit[:, :, :],
                                             n.brb[:, :].unsqueeze(1).to_broadcast([P, NT, E]), ALU.add))
                top, pick = small[4], small[5]
                link(nc.vector.reduce_max(top[:, :], logit[:, :, :], AX.X))
                topb = top[:, :].unsqueeze(2).to_broadcast([P, NT, E])
                link(nc.vector.tensor_tensor(other[:, :, :], logit[:, :, :], topb, ALU.is_equal))
                rampb = n.c("ramp").unsqueeze(1).to_broadcast([P, NT, E])
                link(nc.vector.tensor_tensor(other[:, :, :], other[:, :, :], rampb, ALU.mult))
                link(nc.vector.reduce_max(pick[:, :], other[:, :, :], AX.X))
                nc.vector.tensor_tensor(onehot[:, :, :], pick[:, :].unsqueeze(2).to_broadcast([P, NT, E]),
                                        rampb, ALU.is_equal).then_inc(onehot_ready, 1)
                nc.vector.tensor_tensor(logit[:, :, :], logit[:, :, :], topb, ALU.subtract).then_inc(shifted, 1)
                dve.wait_ge(exp_done, 1)
                link(nc.vector.reduce_sum(top[:, :], logit[:, :, :], AX.X))
                link(nc.vector.reciprocal(top[:, :], top[:, :]))
                link(nc.vector.tensor_scalar(n.tok[:, :, HALF_GATE], top[:, :], 0.5, None, ALU.mult))
                dve.wait_ge(ranks_done, 2)
                link(nc.vector.tensor_copy(cnt[:, :], psC[:, :]))
                wide = other[:, :, :].rearrange("p n e -> p (n e)").rearrange("p (e n) -> p e n", e=E)
                link(nc.vector.tensor_tensor(wide, cnt[:, :].unsqueeze(2).to_broadcast([P, E, NT]),
                                             n.c("full").unsqueeze(1).to_broadcast([P, E, NT]), ALU.is_gt))
                link(nc.vector.reduce_sum(ntile[:, :], wide, AX.X))
                tri = other[:, 0:E, :]
                link(nc.vector.tensor_tensor(tri, n.c("tri").rearrange("p (a b) -> p a b", a=E),
                                             ntile[:, :].unsqueeze(1).to_broadcast([P, E, E]), ALU.mult))
                link(nc.vector.reduce_sum(first[:, :], tri, AX.X))
                link(nc.vector.scalar_tensor_tensor(rank[:, :, :],
                                                    first[:, :].unsqueeze(1).to_broadcast([P, NT, E]), float(P),
                                                    psR[:, :, :], ALU.mult, ALU.add))
                link(nc.vector.tensor_tensor(rank[:, :, :], rank[:, :, :], onehot[:, :, :], ALU.mult))
                link(nc.vector.reduce_sum(pick[:, :], rank[:, :, :], AX.X))
                nc.vector.tensor_copy(pos[:, :], pick[:, :]).then_inc(pos_ready, 1)
                link(nc.vector.tensor_tensor(first[:, :], first[:, :], ntile[:, :], ALU.add))
                link(nc.vector.tensor_tensor(te[:, :, :], first[0:1, :].unsqueeze(1).to_broadcast([1, NS, E]),
                                             n.c("tile", 1).unsqueeze(2).to_broadcast([1, NS, E]), ALU.is_le))
                link(nc.vector.reduce_sum(tef[:, :], te[:, :, :], AX.X))
                link(nc.vector.tensor_scalar(tef[:, :], tef[:, :], float(E - 1), None, ALU.min))
                link(nc.vector.tensor_copy(tile_expert[:, :], tef[:, :]))

            @block.tensor
            def _(pe):
                def router(g):
                    pe.wait_ge(turned_copied, g + 1)
                    for k in range(4):
                        nc.tensor.matmul(psL[:, 4 * g + k, :], xT[g % 2][:, k * P:(k + 1) * P], n.wr[:, :],
                                         start=True, stop=True).then_inc(logits_done, 1)

                pe.wait_ge(n.table_loaded, 16)
                pe.wait_ge(n.router_loaded, 16 * 3)
                for g in range(NCHK):
                    if g >= 2:
                        pe.wait_ge(turned_copied, g - 1)
                    for k in range(4):
                        pe.wait_ge(normed, 4 * g + k + 1)
                        nc.tensor.transpose(psT[g % 2][:, k * P:(k + 1) * P], n.shared[:, 4 * g + k, :],
                                            n.c("ident")).then_inc(turned, 1)
                    if g >= 1:
                        router(g - 1)
                router(NCHK - 1)
                pe.wait_ge(tables_rounded, 1)
                pe.wait_ge(onehot_ready, 1)
                nc.tensor.matmul(psR[:, :, :], n.beforeb[:, :], onehot[:, :, :], start=True, stop=False)
                for k in range(1, NT):
                    last = nc.tensor.matmul(psR[:, k:NT, :], n.onesb[:, :], onehot[:, 0:NT - k, :],
                                            start=False, stop=(k == NT - 1))
                last.then_inc(ranks_done, 1)
                for k in range(NT):
                    last = nc.tensor.matmul(psC[:, :], n.onesb[:, :], onehot[:, k, :],
                                            start=(k == 0), stop=(k == NT - 1))
                last.then_inc(ranks_done, 1)

            @block.scalar
            def _(act):
                act.wait_ge(n.table_loaded, 16)
                nc.scalar.activation(n.identb[:, :], n.c("ident"), ACT.Copy)
                nc.scalar.activation(n.beforeb[:, :], n.c("before"), ACT.Copy).then_inc(tables_rounded, 1)
                for turn in (1, 2):
                    root_of(nc, act, small[4], small[3], square_ready, root_ready, turn)
                for g in range(NCHK):
                    act.wait_ge(turned, 4 * (g + 1))
                    if g >= 2:
                        act.wait_ge(logits_done, 4 * (g - 1))
                    nc.scalar.activation(xT[g % 2][:, :], psT[g % 2][:, :], ACT.Copy).then_inc(turned_copied, 1)
                act.wait_ge(shifted, 1)
                nc.scalar.activation(lg[0][:, :, :], lg[0][:, :, :], ACT.Exp).then_inc(exp_done, 1)

            @block.gpsimd
            def _(pool):
                if r == 0:
                    first_block_pool(nc, pool, n)
                    pool.wait_ge(n.numbered, 1)
                pool.wait_ge(n.blanks_written[r], 16 * (NS // CLEAR))
                pool.wait_ge(pos_ready, 1)
                for t in range(NT):
                    pool.indirect_dma_start(
                        out=n.sort_dram[r][:, :],
                        out_offset=bass.IndirectOffsetOnAxis(ap=pos[:, t:t + 1], axis=0),
                        in_=n.tok[:, t, :], in_offset=None).then_inc(scattered, 16)
                pool.wait_ge(scattered, 16 * NT)

            if r == 0:
                @block.sync
                def _(sp):
                    write_blanks(sp, n)

        with ExitStack() as ctx:
            def sem(name):
                return ctx.enter_context(nc.semaphore(f"g{r}_{name}"))

            def psum(name, width):
                return ctx.enter_context(nc.psum_tensor(f"g{r}_{name}", [P, width], F32))

            def ring(name, count, width):
                return [ctx.enter_context(nc.sbuf_tensor(f"g{r}_{name}{i}", [P, width], F32)) for i in range(count)]

            row = ring("row", LR, TW)
            xnT = ring("xnT", 2, P)
            hid, hidT = ring("hid", 2, F), ring("hidT", 2, F)
            yb, ys = ring("yb", 2, D), ring("ys", 4, D)
            w1s, w2s = ring("w1s", 4, W1W), ring("w2s", 4, W2W)
            psX, psH, psY = ([psum(f"{k}{i}", w) for i in range(2)] for k, w in (("psX", P), ("psH", F), ("psY", D)))
            gate = ctx.enter_context(nc.sbuf_tensor(f"g{r}_gate", [1, 2], F32))
            gate_ready, gated = sem("gate_ready"), sem("gated")
            loaded = [sem(f"loaded{i}") for i in range(LR)]
            y_stored = [sem(f"y_stored{i}") for i in range(LR)]
            x_turned, x_ready, w1_ready, w2_ready, h_done, h_biased, h_ready, y_done, y_biased, y_ready = (
                sem(k) for k in ("x_turned", "x_ready", "w1_ready", "w2_ready", "h_done", "h_biased",
                                 "h_ready", "y_done", "y_biased", "y_ready"))
            block = ctx.enter_context(nc.Block())

            def run(eng, step):
                for t in range(-2, LR):
                    step(t, t % LR)
                with steps(eng, LR, NS - LR, LR) as t:
                    for k in range(LR):
                        step(t + k, k)
                for t in range(NS - LR, NS + 3):
                    step(t, t % LR)

            def there(t):
                return not isinstance(t, int) or 0 <= t < NS

            def expert_of(eng, t):
                return eng.value_load(tile_expert[0:1, ds(t, 1)], min_val=0, max_val=E - 1)

            @block.sync
            def _(sp):
                def load(t, k):
                    if there(t):
                        wait(sp, y_stored[k], (t - k) * (16 // LR))
                        sp.dma_start(row[k][:, :], n.sort_dram[r][ds(t * P, P), :]).then_inc(loaded[k], 16)

                run(sp, load)

            @block.tensor
            def _(pe):
                def turn_x(t, k):
                    if there(t):
                        pe.wait_ge(loaded[k], (t - k) * (16 // LR) + 16)
                        wait(pe, x_ready, t - 1)
                        nc.tensor.transpose(psX[k % 2][:, :], row[k][:, D:2 * D], n.c("ident")).then_inc(x_turned, 1)

                def hidden(t, k):
                    if there(t):
                        pe.wait_ge(x_ready, t + 1)
                        pe.wait_ge(w1_ready, t + 1)
                        wait(pe, h_biased, t - 1)
                        for f in range(FB):
                            last = nc.tensor.matmul(psH[k % 2][:, f * P:(f + 1) * P], w1s[k % 4][:, f * P:(f + 1) * P],
                                                    xnT[k % 2][:, :], start=True, stop=True)
                        last.then_inc(h_done, 1)

                def result(t, k):
                    if there(t):
                        pe.wait_ge(h_ready, t + 1)
                        pe.wait_ge(w2_ready, t + 1)
                        wait(pe, y_biased, t - 1)
                        for f in range(FB):
                            last = nc.tensor.matmul(psY[k % 2][:, :], hidT[k % 2][:, f * P:(f + 1) * P],
                                                    w2s[k % 4][:, f * D:(f + 1) * D], start=(f == 0), stop=(f == FB - 1))
                        last.then_inc(y_done, 1)

                def step(t, k):
                    hidden(t, k)
                    turn_x(t + 1, (k + 1) % LR)
                    result(t - 1, (k - 1) % LR)

                run(pe, step)

            @block.scalar
            def _(act):
                def x_copy(t, k):
                    if there(t):
                        act.wait_ge(x_turned, t + 1)
                        wait(act, h_done, t - 1)
                        nc.scalar.activation(xnT[k % 2][:, :], psX[k % 2][:, :], ACT.Identity,
                                             bias=n.gb[:, 1:2], scale=n.gb[:, 0:1]).then_inc(x_ready, 1)

                def relu(t, k):
                    if there(t):
                        act.wait_ge(h_biased, t + 1)
                        wait(act, y_done, t - 1)
                        nc.scalar.activation(hidT[k % 2][:, :], hid[k % 2][:, :], ACT.Relu).then_inc(h_ready, 1)

                def second_weights(t, k):
                    if there(t):
                        e = expert_of(act, t)
                        wait(act, y_biased, t - 3)
                        nc.scalar.activation(w2s[k % 4][:, :], n.w2[:, ds(e, 1), :], ACT.Copy).then_inc(w2_ready, 1)

                def step(t, k):
                    x_copy(t + 1, (k + 1) % LR)
                    relu(t, k)
                    second_weights(t + 1, (k + 1) % LR)

                run(act, step)

            @block.vector
            def _(dve):
                def first_weights(t, k):
                    if there(t):
                        e = expert_of(dve, t)
                        wait(dve, h_done, t - 3)
                        nc.vector.tensor_copy(w1s[k % 4][:, :], n.w1[:, ds(e, 1), :]).then_inc(w1_ready, 1)

                def bias_hidden(t, k):
                    if there(t):
                        dve.wait_ge(h_done, t + 1)
                        wait(dve, h_ready, t - 1)
                        nc.vector.tensor_tensor(
                            hid[k % 2][:, :].rearrange("p (f t) -> p f t", f=FB),
                            psH[k % 2][:, :].rearrange("p (f t) -> p f t", f=FB),
                            w1s[k % 4][:, F:].unsqueeze(2).to_broadcast([P, FB, P]), ALU.add).then_inc(h_biased, 1)

                def weigh(t, k):
                    if there(t):
                        dve.wait_ge(y_done, t + 1)
                        nc.vector.tensor_tensor(yb[k % 2][:, :], psY[k % 2][:, :], w2s[k % 4][:, FB * D:],
                                                ALU.add).then_inc(y_biased, 1)

                def add_x(t, k):
                    if there(t):
                        if not (isinstance(t, int) and t < 4):
                            before = (k - 4) % LR
                            dve.wait_ge(y_stored[before], (t - 4 - before) * (16 // LR) + 16)
                        dve.wait_ge(y_biased, t + 1)
                        nc.vector.scalar_tensor_tensor(ys[k % 4][:, :], yb[k % 2][:, :], row[k][:, HALF_GATE:HALF_GATE + 1],
                                                       row[k][:, 0:D], ALU.mult, ALU.add).then_inc(y_ready, 1)

                def step(t, k):
                    bias_hidden(t, k)
                    weigh(t - 1, (k - 1) % LR)
                    first_weights(t + 2, (k + 2) % LR)
                    add_x(t - 1, (k - 1) % LR)

                run(dve, step)

            @block.gpsimd
            def _(pool):
                def back(t, k):
                    if there(t):
                        wait(pool, gated, t)
                        pool.wait_ge(y_ready, t + 1)
                        nc.gpsimd.tensor_tensor(gate[:, 0:1], gate[:, 1:2], gate[:, 1:2], ALU.add).then_inc(gated, 1)
                        pool.indirect_dma_start(
                            out=target, out_offset=bass.IndirectOffsetOnAxis(
                                ap=row[k][:, NUMBER:NUMBER + 1].bitcast(U32), axis=0),
                            in_=ys[k % 4][:, :], in_offset=None, bounds_check=B * S - 1,
                            oob_is_err=False).then_inc(y_stored[k], 16)

                nc.gpsimd.memset(gate[:, :], 0.0).then_inc(gate_ready, 1)
                pool.wait_ge(gate_ready, 1)
                run(pool, lambda t, k: back(t - 1, (k - 1) % LR))
                for k in range(LR):
                    pool.wait_ge(y_stored[k], 16 * (NS // LR))


def project(nc, n):
    NC8 = B * NCH
    QB = H // QH
    with ExitStack() as ctx:
        def sb(name, shape, dt=F32):
            return ctx.enter_context(nc.sbuf_tensor(f"p_{name}", shape, dt))

        def psum(name):
            return ctx.enter_context(nc.psum_tensor(f"p_{name}", [P, CH], F32))

        def sem(name):
            return ctx.enter_context(nc.semaphore(f"p_{name}"))

        small = [sb(f"small{i}", [P, NT]) for i in range(3)]
        an = [sb(f"an{i}", [P, CB, D]) for i in range(2)]
        anT = [sb(f"anT{i}", [P, CH]) for i in range(2)]
        rot = [[sb(f"rot{i}{k}", [P, CH]) for k in range(2)] for i in range(2)]
        tmp = [[sb(f"tmp{i}{k}", [P, CH]) for k in range(2)] for i in range(2)]
        rest = [[sb(f"rest{i}{k}", [P, CH]) for k in range(2)] for i in range(2)]
        part = [[[sb(f"part{i}{k}{m}", [P, CH], BF16) for m in range(KINDS)] for k in range(2)] for i in range(2)]
        psA, psV = psum("psA"), psum("psV")
        psP = [[psum(f"psP{i}{k}") for k in range(2)] for i in range(2)]
        stat_done, chain, square_ready, root_ready, normed, turned, turned_copied, v_done, v_copied = (
            sem(k) for k in ("stat_done", "chain", "square_ready", "root_ready", "normed", "turned",
                             "turned_copied", "v_done", "v_copied"))
        proj_done, rotated, summed, hi_done, rest_done, mid_done, lo_done = (
            [sem(f"{k}{i}") for i in range(2)] for k in (
                "proj_done", "rotated", "summed", "hi_done", "rest_done", "mid_done", "lo_done"))
        x_back = [sem(f"x_back{b}") for b in range(B)]
        split_stored = [[sem(f"split_stored{i}{k}") for k in range(2)] for i in range(2)]
        block = ctx.enter_context(nc.Block())

        @block.vector
        def _(dve):
            link = Chain(dve, chain)
            token_stats(nc, dve, n, stat_done, link, x_back)
            rsqrt(nc, dve, link, n.rstd, n.var[:, :], *small, square_ready, root_ready, 1)

            def normalise(g, k):
                wait(dve, turned, g - 1)
                for j in range(CB):
                    last = nc.vector.tensor_scalar(an[k][:, j, :], n.tok[:, ds(g * CB + j, 1), 0:D],
                                                   n.mean[:, ds(g * CB + j, 1)], n.rstd[:, ds(g * CB + j, 1)],
                                                   ALU.subtract, ALU.mult)
                last.then_inc(normed, 1)

            def rotate(g, k):
                for i in range(2):
                    dve.wait_ge(proj_done[i], g + 1)
                    wait(dve, lo_done[i], g - 1)
                    nc.vector.tensor_tensor(rot[i][k][:, :], psP[i][0][:, :], n.c("cos")[:, k * CH:(k + 1) * CH],
                                            ALU.mult)
                    nc.vector.tensor_tensor(tmp[i][k][:, :], psP[i][1][:, :], n.c("sin")[:, k * CH:(k + 1) * CH],
                                            ALU.mult).then_inc(rotated[i], 1)

            def subtract_hi(g, k):
                for i in range(2):
                    dve.wait_ge(hi_done[i], g + 1)
                    nc.vector.tensor_tensor(rest[i][k][:, :], rot[i][k][:, :], part[i][k][0][:, :],
                                            ALU.subtract).then_inc(rest_done[i], 1)

            normalise(0, 0)
            normalise(1, 1)
            rotate(0, 0)
            normalise(2, 0)
            rotate(1, 1)
            subtract_hi(0, 0)
            normalise(3, 1)
            with steps(dve, 2, NC8 - 2, 2) as g:
                rotate(g, 0)
                subtract_hi(g - 1, 1)
                normalise(g + 2, 0)
                rotate(g + 1, 1)
                subtract_hi(g, 0)
                normalise(g + 3, 1)
            rotate(NC8 - 2, 0)
            subtract_hi(NC8 - 3, 1)
            rotate(NC8 - 1, 1)
            subtract_hi(NC8 - 2, 0)
            subtract_hi(NC8 - 1, 1)

        @block.tensor
        def _(pe):
            def turn(g, k):
                pe.wait_ge(normed, g + 1)
                wait(pe, turned_copied, g)
                for j in range(CB):
                    last = nc.tensor.transpose(psA[:, j * P:(j + 1) * P], an[k][:, j, :], n.c("ident"))
                last.then_inc(turned, 1)

            def products(g, k):
                pe.wait_ge(turned_copied, g + 1)
                for i in range(2):
                    wait(pe, rotated[i], g)
                    for m in range(2):
                        last = nc.tensor.matmul(psP[i][m][:, :], n.wproj[:, 2 * i + m, :], anT[k][:, :],
                                                start=True, stop=True)
                    last.then_inc(proj_done[i], 1)
                wait(pe, v_copied, g)
                for j in range(CB):
                    last = nc.tensor.matmul(psV[:, j * P:(j + 1) * P], anT[k][:, j * P:(j + 1) * P],
                                            n.wproj[:, 4, :], start=True, stop=True)
                last.then_inc(v_done, 1)

            turn(0, 0)
            turn(1, 1)
            products(0, 0)
            turn(2, 0)
            products(1, 1)
            with steps(pe, 2, NC8 - 2, 2) as g:
                turn(g + 1, 1)
                products(g, 0)
                turn(g + 2, 0)
                products(g + 1, 1)
            turn(NC8 - 1, 1)
            products(NC8 - 2, 0)
            products(NC8 - 1, 1)

        @block.scalar
        def _(act):
            root_of(nc, act, small[1], small[0], square_ready, root_ready, 1)

            def copy_turned(g, k):
                act.wait_ge(turned, g + 1)
                wait(act, v_done, g - 1)
                nc.scalar.activation(anT[k][:, :], psA[:, :], ACT.Copy).then_inc(turned_copied, 1)

            def values_and_hi(g, k):
                act.wait_ge(v_done, g + 1)
                nc.scalar.activation(n.vals[:, ds((g - k) * 2, QB), k * CB:(k + 1) * CB, :],
                                     psV[:, :].rearrange("p (j q r) -> p q j r", j=CB, q=QB),
                                     ACT.Copy).then_inc(v_copied, 1)
                for i in range(2):
                    act.wait_ge(summed[i], g + 1)
                    wait(act, split_stored[i][k], 16 * KINDS // 2 * (g - k))
                    nc.scalar.activation(part[i][k][0][:, :], rot[i][k][:, :], ACT.Copy).then_inc(hi_done[i], 1)

            def mid(g, k):
                for i in range(2):
                    act.wait_ge(rest_done[i], g + 1)
                    nc.scalar.activation(part[i][k][1][:, :], rest[i][k][:, :], ACT.Copy).then_inc(mid_done[i], 1)

            copy_turned(0, 0)
            copy_turned(1, 1)
            values_and_hi(0, 0)
            copy_turned(2, 0)
            values_and_hi(1, 1)
            mid(0, 0)
            with steps(act, 2, NC8 - 2, 2) as g:
                copy_turned(g + 1, 1)
                values_and_hi(g, 0)
                mid(g - 1, 1)
                copy_turned(g + 2, 0)
                values_and_hi(g + 1, 1)
                mid(g, 0)
            copy_turned(NC8 - 1, 1)
            values_and_hi(NC8 - 2, 0)
            mid(NC8 - 3, 1)
            values_and_hi(NC8 - 1, 1)
            mid(NC8 - 2, 0)
            mid(NC8 - 1, 1)

        @block.gpsimd
        def _(pool):
            def add_pairs(g, k):
                for i in range(2):
                    pool.wait_ge(rotated[i], g + 1)
                    nc.gpsimd.tensor_tensor(rot[i][k][:, :], rot[i][k][:, :], tmp[i][k][:, :],
                                            ALU.add).then_inc(summed[i], 1)

            def subtract_mid(g, k):
                for i in range(2):
                    pool.wait_ge(mid_done[i], g + 1)
                    nc.gpsimd.tensor_tensor(part[i][k][2][:, :], rest[i][k][:, :], part[i][k][1][:, :],
                                            ALU.subtract).then_inc(lo_done[i], 1)

            add_pairs(0, 0)
            add_pairs(1, 1)
            with steps(pool, 2, NC8, 2) as g:
                for k in range(2):
                    subtract_mid(g - 2 + k, k)
                    add_pairs(g + k, k)
            subtract_mid(NC8 - 2, 0)
            subtract_mid(NC8 - 1, 1)

        @block.sync
        def _(sp):
            for b in range(B):
                sp.dma_start(n.tok[:, b * TB:(b + 1) * TB, 0:D],
                             n.x_dram[b * S:(b + 1) * S, :].rearrange("(n p) d -> p n d", p=P)).then_inc(x_back[b], 16)
            with steps(sp, 0, NC8, 2) as g:
                for k in range(2):
                    for i in range(2):
                        sp.wait_ge(lo_done[i], g + k + 1)
                        for m in range(KINDS):
                            rows = slice(m * DK, (m + 1) * DK)
                            if i == 0:
                                there = n.q_dram[rows, k, ds(g * (H // 2), H), :]
                            else:
                                there = n.k_dram[rows, ds(g * (H // 2), H), k * CH:(k + 1) * CH]
                            sp.dma_start(there.rearrange("d h t -> h d t"),
                                         part[i][k][m][:, :]).then_inc(split_stored[i][k], 16)
            for i in range(2):
                for k in range(2):
                    sp.wait_ge(split_stored[i][k], 16 * KINDS * NC8 // 2)


def attention(nc, n):
    units = []
    for ch in range(NCH):
        for j in range((ch + 1) * CB):
            q0 = max(j * P, ch * CH)
            units.append((ch, j, q0, (ch + 1) * CH - q0))
    UN = len(units)
    SC = UN * QH
    diagonal = [u for u, (ch, j, q0, w) in enumerate(units) if j * P == q0]
    half_start = [0, CB]
    half_end = [CB, UN]
    tiles = [((h, h + 1), i) for i in range(CB) for h in range(0, QH, 2)]
    HALF_TILES = len(tiles)
    tiles += [((h,), i) for i in range(CB, TB) for h in range(QH)]
    MT = len(tiles)

    tile_cost = [len(heads) * (i + 1) * P + 120 for heads, i in tiles]
    tile_total = sum(tile_cost)
    att_total = sum(2 * w * QH for _, _, _, w in units)

    def plan(first, last):
        found, att, tile = [], 0, 0

        def spread():
            nonlocal tile
            while not last and tile < MT and sum(tile_cost[:tile + 1]) * att_total <= att * tile_total + AHEAD:
                found.append(("tile", tile, 0))
                tile += 1

        for u in range(UN):
            w = units[u][3]
            for h in range(QH):
                found.append(("score", u, h))
                att += w
                if h == 1:
                    if u >= LAG:
                        found.append(("weigh", u - LAG, 0))
                        att += QH * units[u - LAG][3]
                    elif not first:
                        found.append(("weigh", u - LAG, 1))
                        att += QH * units[u - LAG + UN][3]
                spread()
            for at, what, arg, there in EXTRAS:
                if at == u and (there or not (first if arg == 1 and what == "turn_out" else last)):
                    found.append((what, arg, 0))
        att = att_total * 2
        spread()
        return found

    def uses(first, last):
        return [(0, what, arg) for what, arg, _ in plan(first, last) if what in ("tile", "turn_max", "turn_out")]

    LAG = 2
    AHEAD = tile_total * tile_cost[0] // 2
    EXTRAS = [(1, "turn_max", 1, True), (3, "turn_out", 1, False), (7, "turn_out", 0, True),
              (8, "turn_max", 0, False)]
    before_loop = [(0, "tile", t) for t in range(MT // 2)] + [(0, "turn_max", 0)]
    before_loop += [(0, "tile", t) for t in range(MT // 2, MT)]
    USES = len(uses(False, False))

    def base(s, first):
        return len(before_loop) if first else len(before_loop) + len(uses(True, False)) + (s - 1) * USES

    PARITY = base(1, False) % 2
    assert USES % 2 == 0

    def q_col(h, q):
        return (q // CH * QH + h) * CH + q % CH

    with ExitStack() as ctx:
        def sb(name, shape, dt=F32):
            return ctx.enter_context(nc.sbuf_tensor(f"a_{name}", shape, dt))

        def psum(name, width):
            return ctx.enter_context(nc.psum_tensor(f"a_{name}", [P, width], F32))

        def sem(name):
            return ctx.enter_context(nc.semaphore(f"a_{name}"))

        qs = [sb(f"qs{i}", [PR + MR, QH * S], BF16) for i in range(RING)]
        ks, vs = n.ks, n.vs
        MP = KINDS * QH * CB
        prob = sb("prob", [P, RING, QH, CH])
        rowmax = sb("rowmax", [P, QH, TB])
        maxparts = sb("maxparts", [P, P], BF16)
        maxrest = [sb(f"maxrest{i}", [P, QH, CB]) for i in range(2)]
        maxT = [sb(f"maxT{i}", [MP, P], BF16) for i in range(2)]
        zeros = sb("zeros", [P, QH, CB])
        gate = sb("gate", [1, UN])
        outT = sb("outT", [P, CH])
        recip = [sb(f"recip{i}", [P, CB, QH]) for i in range(NCH)]
        psST = [psum(f"psST{i}", CH) for i in range(3)]
        psS = [psum(f"psS{i}", 2 * CH) for i in range(2)]
        psO = psum("psO", CH)
        maxpart = maxparts[:, 0:MP].rearrange("p (k h i) -> p k h i", k=KINDS, h=QH)
        QB = H // QH

        (cleared, v_ready, scored, use_done, use_read, exp_done, masked, pv_done, out_copied, split_done,
         maxT_ready, split_chain, out_read) = (sem(k) for k in (
             "cleared", "v_ready", "scored", "use_done", "use_read", "exp_done", "masked", "pv_done",
             "out_copied", "split_done", "maxT_ready", "split_chain", "out_read"))
        stack_loaded = [sem(f"stack_loaded{i}") for i in range(RING)]
        max_loaded = [sem(f"max_loaded{i}") for i in range(2)]
        STACK_DMAS = 1 + KINDS * NCH
        block = ctx.enter_context(nc.Block())

        def run(eng, stage):
            stage(0, 0, 0, True, False)
            with eng.Fori(0, (NST - 4) // RING) as i:
                for k in range(1, RING + 1):
                    stage(i * RING + k, k % RING, i + k // RING, False, False)
            for s in range(NST - RING, NST):
                stage(s, s % RING, s // RING, False, s == NST - 1)

        @block.sync
        def _(sp):
            def load(s, r):
                wait(sp, scored, (s - RING + 1) * SC)
                sp.dma_start(ks[r][0:PR, :], n.k_dram[:, ds(s * QH, QH), :].rearrange("d h t -> d (h t)")
                             .unsqueeze(0).to_broadcast([KINDS, KINDS * DK, QH * S])).then_inc(stack_loaded[r], 16)
                for ch in range(NCH):
                    for kind in range(KINDS):
                        sp.dma_start(qs[r][kind * KINDS * DK:(kind + 1) * KINDS * DK,
                                           ch * QH * CH:(ch + 1) * QH * CH],
                                     n.q_dram[kind * DK:(kind + 1) * DK, ch, ds(s * QH, QH), :]
                                     .rearrange("d h t -> d (h t)").unsqueeze(0)
                                     .to_broadcast([KINDS, DK, QH * CH])).then_inc(stack_loaded[r], 16)

            def load_max(s, r, half):
                sp.wait_ge(maxT_ready, 2 * s + half + 1)
                sp.dma_start(qs[r][PR:PR + MR, half * QH * CH:(half + 1) * QH * CH],
                             maxT[half][:, :]).then_inc(max_loaded[half], 16)

            def stage(s, r, turn, first, last):
                if not first and not last and not (isinstance(s, int) and s + 2 >= NST):
                    load(s + 2, (r + 2) % RING)
                load_max(s, r, 1)
                if not last:
                    load_max(s + 1, (r + 1) % RING, 0)

            load(0, 0)
            load(1, 1)
            load_max(0, 0, 0)
            load(2, 2)
            run(sp, stage)

        @block.tensor
        def _(pe):
            def use(index):
                wait(pe, use_read, index - 1)

            def tile(r, turn, t, index, ps):
                heads, i = tiles[t]
                if t == 0:
                    pe.wait_ge(stack_loaded[r], (turn + 1) * 16 * STACK_DMAS)
                use(index)
                width = (i + 1) * P
                for a, h in enumerate(heads):
                    lhs = qs[r][0:PR, q_col(h, i * P):q_col(h, i * P) + P]
                    for c0 in range(0, width, CH):
                        w = min(CH, width - c0)
                        nc.tensor.matmul(ps[:, a * CH + c0:a * CH + c0 + w], lhs,
                                         ks[r][0:PR, h * S + c0:h * S + c0 + w], start=True, stop=c0 + w < width)
                    last = nc.tensor.matmul(ps[:, a * CH + i * P:a * CH + width], n.identb[:, :], n.maskb[:, :],
                                            start=False, stop=True)
                last.then_inc(use_done, 1)

            def turn_max(s, half, index, ps):
                use(index)
                pe.wait_ge(split_done, 2 * s + half + 1)
                nc.tensor.transpose(ps[:, 0:P // 2].bitcast(BF16), maxparts[:, :], n.identb[:, :]).then_inc(use_done, 1)

            def turn_out(s, ch, index, ps):
                use(index)
                pe.wait_ge(out_copied, 2 * s + ch + 1)
                for b in range(CB):
                    last = nc.tensor.transpose(ps[:, b * P:(b + 1) * P], outT[:, b * P:(b + 1) * P], n.c("ident"))
                last.then_inc(use_done, 1)

            def score(s, r, u, h):
                ch, j, q0, w = units[u]
                if u in half_start and h == 0:
                    half = half_start.index(u)
                    pe.wait_ge(max_loaded[half], (s + 1) * 16)
                wait(pe, exp_done, s * SC + u * QH + h - 2)
                nc.tensor.matmul(psST[(u * QH + h) % 3][:, 0:w], ks[r][:, h * S + j * P:h * S + (j + 1) * P],
                                 qs[r][:, q_col(h, q0):q_col(h, q0) + w], start=True, stop=True).then_inc(scored, 1)

            def weigh(s, r, u):
                ch, j, q0, w = units[u]
                pe.wait_ge(exp_done, s * SC + (u + 1) * QH)
                if u in diagonal:
                    pe.wait_ge(masked, s * len(diagonal) + diagonal.index(u) + 1)
                if u in half_start:
                    pe.wait_ge(v_ready, s + 1)
                    wait(pe, out_copied, 2 * s + half_start.index(u))
                c0 = q0 - ch * CH
                for h in range(QH):
                    last = nc.tensor.matmul(psO[32 * h:32 * h + 32, c0:c0 + w], vs[r][:, j, h, :],
                                            prob[:, u % RING, h, 0:w], start=(j == 0),
                                            stop=(u + 1 in half_end))
                last.then_inc(pv_done, 1)

            def stage(s, r, turn, first, last):
                b, parity = base(s, first), base(0, True) % 2 if first else PARITY
                k = 0
                for what, arg, arg2 in plan(first, last):
                    if what == "score":
                        score(s, r, arg, arg2)
                        continue
                    if what == "weigh":
                        if arg2:
                            weigh(s - 1, (r - 1) % RING, arg + UN)
                        else:
                            weigh(s, r, arg)
                        continue
                    ps = psS[(parity + k) % 2]
                    if what == "tile":
                        tile((r + 1) % RING, turn + (r + 1) // RING, arg, b + k, ps)
                    elif what == "turn_max":
                        turn_max(s if arg else s + 1, arg, b + k, ps)
                    else:
                        turn_out(s - 1 if arg else s, arg, b + k, ps)
                    k += 1

            for k, (_, what, arg) in enumerate(before_loop):
                if what == "tile":
                    tile(0, 0, arg, k, psS[k % 2])
                else:
                    turn_max(0, arg, k, psS[k % 2])
            run(pe, stage)
            weigh(NST - 1, (NST - 1) % RING, UN - 2)
            weigh(NST - 1, (NST - 1) % RING, UN - 1)
            end = base(NST - 1, False) + len(uses(False, True))
            turn_out(NST - 1, 1, end, psS[end % 2])

        @block.scalar
        def _(act):
            def exps(s, u):
                ch, j, q0, w = units[u]
                wait(act, pv_done, s * UN + u - 2)
                for h in range(QH):
                    act.wait_ge(scored, s * SC + u * QH + h + 1)
                    nc.scalar.activation(prob[:, u % RING, h, 0:w], psST[(u * QH + h) % 3][:, 0:w], ACT.Exp,
                                         scale=SCALE).then_inc(exp_done, 1)

            def copy_out(s, ch):
                act.wait_ge(pv_done, s * UN + half_end[ch])
                wait(act, out_read, 2 * s + ch)
                nc.scalar.activation(outT[:, :], psO[:, :], ACT.Copy).then_inc(out_copied, 1)

            def stage(s, r, turn, first, last):
                for u in range(UN):
                    if u == 1 and not first:
                        copy_out(s - 1, 1)
                    if u == half_end[0] + 1:
                        copy_out(s, 0)
                    exps(s, u)

            run(act, stage)
            copy_out(NST - 1, 1)

        @block.vector
        def _(dve):
            nc.vector.memset(maxparts[:, :], 0.0)
            nc.vector.memset(zeros[:, :, :], 0.0).then_inc(cleared, 1)

            def reduce(s, t, index, ps):
                heads, i = tiles[t]
                if t in (0, HALF_TILES):
                    wait(dve, split_done, 2 * s - 1 + (t > 0))
                dve.wait_ge(use_done, index + 1)
                width = (i + 1) * P
                if len(heads) == 2:
                    src = ps[:, :].rearrange("p (a c) -> p a c", a=2)[:, :, 0:width]
                    nc.vector.reduce_max(rowmax[:, heads[0]:heads[0] + 2, i], src, AX.X).then_inc(use_read, 1)
                else:
                    nc.vector.reduce_max(rowmax[:, heads[0]:heads[0] + 1, i], ps[:, 0:width],
                                         AX.X).then_inc(use_read, 1)

            def copy_max(s, half, index, ps):
                dve.wait_ge(use_done, index + 1)
                wait(dve, max_loaded[half], s * 16)
                nc.vector.tensor_copy(maxT[half][:, :],
                                      ps[0:MP, 0:P // 2].bitcast(BF16)).then_inc(use_read, 1)
                dve.wait_ge(use_read, index + 1)
                dve.sem_inc(maxT_ready, 1)

            def normalise(s, ch, index, ps):
                dve.wait_ge(use_done, index + 1)
                src = ps[:, 0:CH].rearrange("p (b h c) -> p b h c", b=CB, h=QH)
                nc.vector.reciprocal(recip[ch][:, :, :], src[:, :, :, DK]).then_inc(out_read, 1)
                dve.wait_ge(out_read, 2 * s + ch + 1)
                nc.vector.tensor_tensor(
                    n.shared[:, ds((s // QB) * TB + ch * CB, CB), ds((s % QB) * RW, RW)]
                    .rearrange("p j (h d) -> p j h d", h=QH),
                    src[:, :, :, 0:DK], recip[ch][:, :, :].unsqueeze(3).to_broadcast([P, CB, QH, DK]),
                    ALU.mult).then_inc(use_read, 1)

            def do(s, what, arg, index, ps):
                if what == "tile":
                    reduce(s + 1, arg, index, ps)
                elif what == "turn_max":
                    copy_max(s if arg else s + 1, arg, index, ps)
                else:
                    normalise(s - 1 if arg else s, arg, index, ps)

            def stage(s, r, turn, first, last):
                b, parity = base(s, first), base(0, True) % 2 if first else PARITY
                for k, (_, what, arg) in enumerate(uses(first, last)):
                    do(s, what, arg, b + k, psS[(parity + k) % 2])

            for k, (_, what, arg) in enumerate(before_loop):
                do(-1, what, arg, k, psS[k % 2])
            run(dve, stage)
            end = base(NST - 1, False) + len(uses(False, True))
            normalise(NST - 1, 1, end, psS[end % 2])

        @block.gpsimd
        def _(pool):
            half_ready = {}
            for what, found in (("first", uses(True, False)), ("middle", uses(False, False))):
                for half, t in ((0, HALF_TILES - 1), (1, MT - 1)):
                    half_ready[what, half] = [k for k, (_, w, a) in enumerate(found) if (w, a) == ("tile", t)][0] + 1
            def split(s, half, count, order):
                pool.wait_ge(use_read, count)
                wait(pool, maxT_ready, 2 * s + half)
                src = rowmax[:, :, half * CB:(half + 1) * CB]
                done = order * 4

                def link(ins, k):
                    ins.then_inc(split_chain, 1)
                    pool.wait_ge(split_chain, done + k)

                zero = zeros[:, :, :]
                link(nc.gpsimd.tensor_tensor(maxpart[:, 0, :, :], zero, src, ALU.subtract), 1)
                link(nc.gpsimd.tensor_tensor(maxrest[0][:, :, :], src, maxpart[:, 0, :, :], ALU.add), 2)
                link(nc.gpsimd.tensor_tensor(maxpart[:, 1, :, :], zero, maxrest[0][:, :, :], ALU.subtract), 3)
                link(nc.gpsimd.tensor_tensor(maxrest[1][:, :, :], maxrest[0][:, :, :], maxpart[:, 1, :, :],
                                             ALU.add), 4)
                nc.gpsimd.tensor_tensor(maxpart[:, 2, :, :], zero, maxrest[1][:, :, :],
                                        ALU.subtract).then_inc(split_done, 1)

            def values(s, r):
                wait(pool, pv_done, (s - RING + 1) * UN + 1)
                nc.gpsimd.tensor_copy(vs[r][:, :, :, 0:DK],
                                      n.vals[:, ds(s, 1), :, :].rearrange("p s j (h d) -> p (s j) h d", h=QH)
                                      ).then_inc(v_ready, 1)

            def mask(s, u):
                pool.wait_ge(exp_done, s * SC + (u + 1) * QH)
                part = prob[:, u % RING, :, 0:P]
                nc.gpsimd.tensor_tensor(gate[:, u:u + 1], zeros[0:1, 0, 0:1], zeros[0:1, 0, 1:2], ALU.add)
                nc.gpsimd.affine_select(out=part, in_=part, compare_op=ALU.is_ge, fill=0.0, base=0,
                                        pattern=[[0, QH], [1, P]], channel_multiplier=-1).then_inc(masked, 1)

            def stage(s, r, turn, first, last):
                for u in diagonal:
                    if u == half_end[0] + CB:
                        if not last:
                            split(s + 1, 0, base(s, first) + half_ready["first" if first else "middle", 0],
                                  2 * s + 2)
                            values(s + 1, (r + 1) % RING)
                    mask(s, u)
                if not last:
                    split(s + 1, 1, base(s, first) + half_ready["first" if first else "middle", 1], 2 * s + 3)

            pool.wait_ge(cleared, 1)
            nc.gpsimd.tensor_copy(vs[0][:, :, :, 0:DK],
                                  n.vals[:, 0, :, :].rearrange("p j (h d) -> p j h d", h=QH)).then_inc(v_ready, 1)
            split(0, 0, HALF_TILES, 0)
            split(0, 1, len(before_loop), 1)
            run(pool, stage)


def output_projection(nc, n):
    QB = H // QH
    G = NT // CB
    with ExitStack() as ctx:
        oT = [ctx.enter_context(nc.sbuf_tensor(f"o_T{i}", [P, CH], F32)) for i in range(2)]
        psT = [ctx.enter_context(nc.psum_tensor(f"o_psT{i}", [P, CH], F32)) for i in range(2)]
        psY = [ctx.enter_context(nc.psum_tensor(f"o_psY{i}", [P, CH], F32)) for i in range(2)]
        turned, turned_copied, projected, added = (ctx.enter_context(nc.semaphore(f"o_{k}")) for k in (
            "turned", "turned_copied", "projected", "added"))
        block = ctx.enter_context(nc.Block())

        @block.tensor
        def _(pe):
            def product(g):
                pe.wait_ge(turned_copied, g + 1)
                wait(pe, added, g - 1)
                for j in range(CB):
                    last = nc.tensor.matmul(psY[g % 2][:, j * P:(j + 1) * P], oT[g % 2][:, j * P:(j + 1) * P],
                                            n.wproj[:, 5, :], start=True, stop=True)
                last.then_inc(projected, 1)

            for g in range(G):
                wait(pe, turned_copied, g - 1)
                for j in range(CB):
                    last = nc.tensor.transpose(psT[g % 2][:, j * P:(j + 1) * P],
                                               n.shared[:, g * CB + j, :], n.c("ident"))
                last.then_inc(turned, 1)
                if g >= 1:
                    product(g - 1)
            product(G - 1)

        @block.scalar
        def _(act):
            for g in range(G):
                act.wait_ge(turned, g + 1)
                wait(act, projected, g - 1)
                nc.scalar.activation(oT[g % 2][:, :], psT[g % 2][:, :], ACT.Copy).then_inc(turned_copied, 1)

        @block.vector
        def _(dve):
            for g in range(G):
                dve.wait_ge(projected, g + 1)
                part = n.tok[:, g * CB:(g + 1) * CB, 0:D]
                nc.vector.tensor_tensor(part, part, psY[g % 2][:, :].rearrange("p (j d) -> p j d", j=CB),
                                        ALU.add).then_inc(added, 1)


_OUT = (B, S, D)


def kernel(**inputs):
    import concourse.bacc as bacc
    from concourse.bass_utils import run_bass_kernel_spmd

    def arr(name):
        return np.ascontiguousarray(inputs[name])

    def swapped(w):
        return w.reshape(D // 2, 2, D)[:, ::-1, :].reshape(D, D)

    wq, wk = arr("L0_attn_Wq"), arr("L0_attn_Wk")
    weights = (wq, swapped(wq), wk, swapped(wk), arr("L0_attn_Wv"), arr("L0_attn_Wo"))
    arrays = {
        "x": arr("L0_attn_x"), "Wp": np.stack([w.T for w in weights], axis=1),
        "Wr": arr("L0_ffn_Wr"), "br": arr("L0_ffn_br"),
        "ln": np.stack([arr("L0_ffn_ln_g"), arr("L0_ffn_ln_b")], axis=1),
        "Wb1": np.concatenate([arr("L0_ffn_W1").transpose(1, 0, 2),
                               arr("L0_ffn_b1").reshape(E, FB, P).transpose(2, 0, 1)], axis=2),
        "W2": np.ascontiguousarray(arr("L0_ffn_W2").reshape(E, FB, P, D).transpose(2, 0, 1, 3).reshape(P, E, FB * D)),
        "b2": arr("L0_ffn_b2"), "const": constants(),
    }
    nc = bacc.Bacc("TRN2", target_bir_lowering=False, num_devices=1)
    args = {k: nc.dram_tensor(f"in_{k}", a.shape, mybir.dt.from_np(a.dtype), kind="ExternalInput").ap()
            for k, a in arrays.items()}
    out = nc.dram_tensor("out_x", _OUT, F32, kind="ExternalOutput").ap()
    build(nc, out=out, **args)
    result = run_bass_kernel_spmd(nc, [{f"in_{k}": a for k, a in arrays.items()}], core_ids=[0])
    return result.results[0]["out_x"]
```

```python
from contextlib import ExitStack, contextmanager

import numpy as np

import concourse.bass as bass
from concourse import mybir

F32 = mybir.dt.float32
BF16 = mybir.dt.bfloat16
U32 = mybir.dt.uint32
I32 = mybir.dt.int32
ALU = mybir.AluOpType
ACT = mybir.ActivationFunctionType
AX = mybir.AxisListType

B, S, D = 4, 1024, 128
H, DK = 16, 8
E, F = 8, 512
P = 128
NT = B * S // P
TB = S // P
FB = F // P
NS = NT + E - 1
EPS = 1e-5
SCALE = DK ** -0.5
NEG = -1e30
QH = 4
NST = B * H // QH
RW = QH * DK
KINDS = 3
PR = KINDS * KINDS * DK
MR = KINDS
CH = 512
NCH = S // CH
CB = CH // P
TW = 2 * D + 1
HALF_GATE = 2 * D
W1W, W2W = F + FB, FB * D + D
LR = 8
WARM = (18, 16)
GATHER_AHEAD = 4
RING = 3

CONST = {}
_at = 0
for _name, _width in (("ident", P), ("before", P), ("mask", P), ("ramp", E), ("full", NT),
                      ("tri", E * E), ("tile", NS), ("slot", P), ("partition", 1), ("earlier", NT), ("cos", S), ("sin", S)):
    CONST[_name] = (_at, _at + _width)
    _at += _width
CONST_W = _at


def constants():
    t = np.zeros((P, CONST_W), np.float32)

    def put(name, a):
        t[:, CONST[name][0]:CONST[name][1]] = a

    i = np.arange(P)
    put("ident", np.eye(P))
    put("before", i[:, None] < i[None, :])
    put("mask", np.where(i[None, :] <= i[:, None], 0.0, NEG))
    put("ramp", np.arange(E, 0, -1))
    put("full", P * np.arange(NT))
    put("tri", (np.arange(E)[None, :] < np.arange(E)[:, None]).reshape(1, -1))
    put("tile", np.arange(NS))
    put("partition", i[:, None])
    put("earlier", np.arange(NT) - NT)
    put("slot", i)
    half = DK // 2
    freq = np.float32(10000.0) ** (-np.arange(0, half, dtype=np.float32) * np.float32(2.0) / np.float32(DK))
    angle = np.arange(S, dtype=np.float32)[None, :] * freq[:, None].astype(np.float32)
    row = (i % DK) // 2
    put("cos", np.cos(angle)[row])
    put("sin", np.sin(angle)[row] * np.where(i % 2 == 0, -1.0, 1.0)[:, None])
    return t


def ds(start, size):
    return bass.ds(start, size)


@contextmanager
def steps(eng, start, end, step):
    with eng.Fori(start // step, end // step) as i:
        yield i * step


def wait(eng, sem, value):
    if isinstance(value, int) and value <= 0:
        return
    eng.wait_ge(sem, value)


class Chain:

    def __init__(self, eng, sem):
        self.eng, self.sem, self.n = eng, sem, 0

    def __call__(self, ins):
        self.n += 1
        ins.then_inc(self.sem, 1)
        self.eng.wait_ge(self.sem, self.n)


class Kept:
    pass


def build(nc, x, Wp, Wr, br, ln, Wb1, W2, b2, const, out):
    ctx = ExitStack()
    with ctx:
        def sb(name, shape, dt=F32):
            return ctx.enter_context(nc.sbuf_tensor(name, shape, dt))

        n = Kept()
        n.x, n.Wp, n.Wr, n.br, n.ln, n.Wb1, n.W2, n.b2, n.const = x, Wp, Wr, br, ln, Wb1, W2, b2, const
        n.tok = sb("tok", [P, NT, TW])
        n.cst = sb("cst", [P, CONST_W])
        n.identb = sb("identb", [P, P], BF16)
        n.beforeb = sb("beforeb", [P, P], BF16)
        n.maskb = sb("maskb", [P, P], BF16)
        n.onesb = sb("onesb", [P, P], BF16)
        n.wproj = sb("wproj", [P, 6, D])
        n.wr = sb("wr", [P, E])
        n.gb = sb("gb", [P, 2])
        n.brb = sb("brb", [P, E])
        n.w1 = sb("w1", [P, E, W1W])
        n.w2 = sb("w2", [P, E, W2W])
        n.mean = sb("mean", [P, NT])
        n.stats = sb("stats", [P, NT, 6])
        n.var = sb("var", [P, NT])
        n.rstd = sb("rstd", [P, NT])
        n.shared = n.tok[:, :, D:2 * D]
        n.vals = sb("vals", [P, NST, TB, RW])

        n.ks = [sb(f"ks{i}", [PR + MR, QH * S], BF16) for i in range(RING)]
        n.qs = [sb("qs0", [PR + MR, QH * S], BF16)]
        n.vs = [sb(f"vs{i}", [P, TB, QH, 32]) for i in range(RING)]

        def c(name, rows=P):
            return n.cst[0:rows, CONST[name][0]:CONST[name][1]]

        n.q_dram = nc.dram_tensor("q_split", (KINDS * DK, NCH, B * H, CH), BF16, kind="Internal").ap()
        n.k_dram = nc.dram_tensor("k_split", (KINDS * DK, B * H, S), BF16, kind="Internal").ap()
        n.rows_dram = [nc.dram_tensor(f"rows{r}", (B * S, TW), F32, kind="Internal").ap() for r in range(2)]
        n.x_dram = nc.dram_tensor("x_after_first", (B * S, D), F32, kind="Internal").ap()

        def sem(name):
            return ctx.enter_context(nc.semaphore(name))

        n.x_loaded = [sem(f"x_loaded{b}") for b in range(B)]
        n.table_loaded, n.router_loaded, n.weights_loaded = sem("table_loaded"), sem("router_loaded"), sem("weights_loaded")
        n.ring_init, n.first_stack_loaded = sem("ring_init"), sem("first_stack_loaded")
        n.c = c
        setup(nc, n)
        ffn(nc, n, 0, n.x_dram)
        attend(nc, n)
        output_projection(nc, n)
        ffn(nc, n, 1, out.rearrange("b s d -> (b s) d"))


HEAD_W = CONST["cos"][0]


def setup(nc, n):
    with ExitStack() as ctx:
        block = ctx.enter_context(nc.Block())

        def load_x(eng, b):
            eng.dma_start(n.tok[:, b * TB:(b + 1) * TB, 0:D],
                          n.x[b].rearrange("(n p) d -> p n d", p=P)).then_inc(n.x_loaded[b], 16)

        @block.sync
        def _(sp):
            load_x(sp, 0)
            load_x(sp, 2)
            sp.dma_start(n.cst[:, 0:HEAD_W], n.const[:, 0:HEAD_W]).then_inc(n.table_loaded, 16)

        @block.scalar
        def _(act):
            load_x(act, 1)
            load_x(act, 3)
            act.dma_start(n.wr[:, :], n.Wr).then_inc(n.router_loaded, 16)
            act.dma_start(n.gb[:, :], n.ln).then_inc(n.router_loaded, 16)
            act.dma_start(n.brb[:, :], n.br.partition_broadcast(P)).then_inc(n.router_loaded, 16)

        @block.vector
        def _(dve):
            nc.vector.memset(n.onesb[:, :], 1.0)


LOADS = 5


def load_weights(sp, n):
    for there, source in ((n.w1[:, :, :], n.Wb1), (n.w2[:, :, 0:FB * D], n.W2),
                          (n.w2[:, :, FB * D:], n.b2.partition_broadcast(P)),
                          (n.cst[:, HEAD_W:], n.const[:, HEAD_W:]), (n.wproj[:, :, :], n.Wp)):
        sp.dma_start(there, source).then_inc(n.weights_loaded, 16)


def first_block_pool(nc, pool, n):
    pool.wait_ge(n.table_loaded, 16)
    link = Chain(pool, n.ring_init)
    link(nc.gpsimd.tensor_copy(n.maskb[:, :], n.c("mask")))
    for r in range(RING):
        link(nc.gpsimd.memset(n.ks[r][64:PR + MR, :], 1.0))
        link(nc.gpsimd.memset(n.vs[r][:, :, :, DK + 1:], 0.0))
        link(nc.gpsimd.memset(n.vs[r][:, :, :, DK:DK + 1], 1.0))


def warm_up(nc, pe, n, ps, times):
    with pe.Fori(0, times) as _:
        for k in range(4):
            nc.tensor.matmul(ps[:, :], n.onesb[:, :], n.onesb[:, :], start=True, stop=True)


MEASURED = None


def token_stats(nc, dve, n, stat_done, link, ready):
    if ready is not MEASURED:
        for t in range(NT):
            if t % TB == 0:
                dve.wait_ge(ready[t // TB], 16)
            nc.vector.bn_stats(n.stats[:, t, :], n.tok[:, t, 0:D]).then_inc(stat_done, 1)
        dve.wait_ge(stat_done, NT)
    mean, var = n.mean[:, :], n.var[:, :]
    even, odd, sq_even, sq_odd = (n.stats[:, :, k] for k in (1, 4, 2, 5))
    link(nc.vector.tensor_tensor(mean, even, odd, ALU.add))
    link(nc.vector.tensor_scalar(mean, mean, 0.5, None, ALU.mult))
    link(nc.vector.tensor_tensor(var, sq_even, sq_odd, ALU.add))
    link(nc.vector.tensor_tensor(even, even, odd, ALU.subtract))
    link(nc.vector.scalar_tensor_tensor(even, even, 0.25, even, ALU.mult, ALU.mult))
    link(nc.vector.scalar_tensor_tensor(var, var, 1.0 / D, even, ALU.mult, ALU.add))


def rsqrt(nc, dve, link, out, var, shifted, root, corr, square_ready, root_ready, turn):
    nc.vector.tensor_scalar(shifted[:, :], var, EPS, None, ALU.add).then_inc(square_ready, 1)
    dve.wait_ge(root_ready, turn)
    link(nc.vector.reciprocal(out[:, :], root[:, :]))
    link(nc.vector.tensor_tensor(corr[:, :], out[:, :], out[:, :], ALU.mult))
    link(nc.vector.tensor_tensor(corr[:, :], corr[:, :], shifted[:, :], ALU.mult))
    link(nc.vector.tensor_scalar(corr[:, :], corr[:, :], -0.5, 1.5, ALU.mult, ALU.add))
    link(nc.vector.tensor_tensor(out[:, :], out[:, :], corr[:, :], ALU.mult))


def root_of(nc, act, root, shifted, square_ready, root_ready, turn):
    act.wait_ge(square_ready, turn)
    nc.scalar.activation(root[:, :], shifted[:, :], ACT.Sqrt).then_inc(root_ready, 1)


def ffn(nc, n, r, target):
    NCHK = NT // 4
    outer = ExitStack()
    with outer:
        def sb(name, shape, dt=F32):
            return outer.enter_context(nc.sbuf_tensor(f"f{r}_{name}", shape, dt))

        number = sb("number", [P, NS], U32)
        there_number = sb("there_number", [P, NS], U32)
        tile_expert = sb("tile_expert", [1, NS], I32)
        small = [sb(f"small{i}", [P, NT]) for i in range(6)]
        lg = [sb(f"lg{i}", [P, NT, E]) for i in range(3)]
        onehot = sb("onehot", [P, NT, E], BF16)
        cnt = sb("cnt", [P, E])
        ntile = sb("ntile", [P, E])
        first = sb("first", [P, E])
        xT = [sb(f"xT{i}", [P, 4 * P]) for i in range(2)]
        te = sb("te", [1, NS, E])
        tef = sb("tef", [1, NS])

        with ExitStack() as ctx:
            def sem(name):
                return ctx.enter_context(nc.semaphore(f"f{r}_{name}"))

            psT = [ctx.enter_context(nc.psum_tensor(f"f{r}_psT{i}", [P, 512], F32)) for i in range(2)]
            psL = ctx.enter_context(nc.psum_tensor(f"f{r}_psL", [P, NT, E], F32))
            psR = ctx.enter_context(nc.psum_tensor(f"f{r}_psR", [P, NT, E], F32))
            psC = ctx.enter_context(nc.psum_tensor(f"f{r}_psC", [P, E], F32))
            psW = ctx.enter_context(nc.psum_tensor(f"f{r}_psW", [P, P], F32))
            slot_is = ctx.enter_context(nc.sbuf_tensor(f"f{r}_slot_is", [P, NT, P], BF16))
            tile_is, tile_lo, tile_hi = (ctx.enter_context(nc.sbuf_tensor(f"f{r}_{k}", [P, NT, NS], BF16))
                                         for k in ("tile_is", "tile_lo", "tile_hi"))
            place = [ctx.enter_context(nc.sbuf_tensor(f"f{r}_place{i}", [P, NT], U32)) for i in range(2)]
            numf = [ctx.enter_context(nc.sbuf_tensor(f"f{r}_numf{i}", [P, NS], F32)) for i in range(2)]
            psN = [ctx.enter_context(nc.psum_tensor(f"f{r}_psN{i}", [P, NS], F32)) for i in range(2)]
            stat_done, chain = sem("stat_done"), sem("chain")
            square_ready, root_ready = sem("square_ready"), sem("root_ready")
            normed, turned, turned_copied, logits_done = (sem("normed"), sem("turned"), sem("turned_copied"),
                                                          sem("logits_done"))
            shifted, exp_done, onehot_ready, ranks_done = (sem("shifted"), sem("exp_done"), sem("onehot_ready"),
                                                           sem("ranks_done"))
            rows_ready, rows_stored, tables_rounded = sem("rows_ready"), sem("rows_stored"), sem("tables_rounded")
            counts_done = sem("counts_done")
            tiles_found, lo_made, slots_found, numbers_done = (sem("tiles_found"), sem("lo_made"),
                                                               sem("slots_found"), sem("numbers_done"))
            block = ctx.enter_context(nc.Block())

            @block.vector
            def _(dve):
                link = Chain(dve, chain)
                token_stats(nc, dve, n, stat_done, link, n.x_loaded if r == 0 else MEASURED)
                rstd_u, scale, inv_u, shift, root, corr = small
                rsqrt(nc, dve, link, n.rstd, n.var[:, :], shift, root, corr, square_ready, root_ready, 1)
                link(nc.vector.tensor_tensor(scale[:, :], n.rstd[:, :], n.rstd[:, :], ALU.mult))
                link(nc.vector.tensor_tensor(scale[:, :], scale[:, :], n.var[:, :], ALU.mult))
                rsqrt(nc, dve, link, rstd_u, scale[:, :], shift, root, corr, square_ready, root_ready, 2)
                link(nc.vector.tensor_tensor(inv_u[:, :], shift[:, :], rstd_u[:, :], ALU.mult))
                link(nc.vector.tensor_tensor(scale[:, :], n.rstd[:, :], rstd_u[:, :], ALU.mult))
                for t in range(NT):
                    nc.vector.tensor_scalar(n.shared[:, t, :], n.tok[:, t, 0:D], n.mean[:, t:t + 1],
                                            scale[:, t:t + 1],
                                            ALU.subtract, ALU.mult).then_inc(normed, 1)
                logit, other, rank = lg
                dve.wait_ge(logits_done, NT)
                dve.wait_ge(n.table_loaded, 16)
                dve.wait_ge(n.router_loaded, 16 * 3)
                link(nc.vector.tensor_tensor(logit[:, :, :], psL[:, :, :],
                                             inv_u[:, :].unsqueeze(2).to_broadcast([P, NT, E]), ALU.mult))
                link(nc.vector.tensor_tensor(logit[:, :, :], logit[:, :, :],
                                             n.brb[:, :].unsqueeze(1).to_broadcast([P, NT, E]), ALU.add))
                top, pick = small[4], small[5]
                link(nc.vector.reduce_max(top[:, :], logit[:, :, :], AX.X))
                topb = top[:, :].unsqueeze(2).to_broadcast([P, NT, E])
                link(nc.vector.tensor_tensor(other[:, :, :], logit[:, :, :], topb, ALU.is_equal))
                rampb = n.c("ramp").unsqueeze(1).to_broadcast([P, NT, E])
                link(nc.vector.tensor_tensor(other[:, :, :], other[:, :, :], rampb, ALU.mult))
                link(nc.vector.reduce_max(pick[:, :], other[:, :, :], AX.X))
                nc.vector.tensor_tensor(onehot[:, :, :], pick[:, :].unsqueeze(2).to_broadcast([P, NT, E]),
                                        rampb, ALU.is_equal).then_inc(onehot_ready, 1)
                nc.vector.tensor_tensor(logit[:, :, :], logit[:, :, :], topb, ALU.subtract).then_inc(shifted, 1)
                dve.wait_ge(exp_done, 1)
                link(nc.vector.reduce_sum(top[:, :], logit[:, :, :], AX.X))
                link(nc.vector.reciprocal(top[:, :], top[:, :]))
                nc.vector.tensor_scalar(n.tok[:, :, HALF_GATE], top[:, :], 0.5, None, ALU.mult).then_inc(rows_ready, 1)
                dve.wait_ge(counts_done, 1)
                link(nc.vector.tensor_copy(cnt[:, :], psC[:, :]))
                wide = other[:, :, :].rearrange("p n e -> p (n e)").rearrange("p (e n) -> p e n", e=E)
                link(nc.vector.tensor_tensor(wide, cnt[:, :].unsqueeze(2).to_broadcast([P, E, NT]),
                                             n.c("full").unsqueeze(1).to_broadcast([P, E, NT]), ALU.is_gt))
                link(nc.vector.reduce_sum(ntile[:, :], wide, AX.X))
                tri = other[:, 0:E, :]
                link(nc.vector.tensor_tensor(tri, n.c("tri").rearrange("p (a b) -> p a b", a=E),
                                             ntile[:, :].unsqueeze(1).to_broadcast([P, E, E]), ALU.mult))
                link(nc.vector.reduce_sum(first[:, :], tri, AX.X))
                slot, tile, base_tile = small[0], small[1], small[2]
                link(nc.vector.tensor_tensor(other[:, :, :], onehot[:, :, :],
                                             first[:, :].unsqueeze(1).to_broadcast([P, NT, E]), ALU.mult))
                link(nc.vector.reduce_sum(base_tile[:, :], other[:, :, :], AX.X))
                dve.wait_ge(ranks_done, 1)
                link(nc.vector.tensor_tensor(rank[:, :, :], psR[:, :, :], onehot[:, :, :], ALU.mult))
                link(nc.vector.reduce_sum(pick[:, :], rank[:, :, :], AX.X))
                link(nc.vector.tensor_copy(place[0][:, :], pick[:, :]))
                link(nc.vector.tensor_scalar(place[1][:, :], place[0][:, :], P - 1, None, ALU.bitwise_and))
                link(nc.vector.tensor_copy(slot[:, :], place[1][:, :]))
                link(nc.vector.tensor_tensor(tile[:, :], pick[:, :], slot[:, :], ALU.subtract))
                link(nc.vector.scalar_tensor_tensor(tile[:, :], tile[:, :], 1.0 / P, base_tile[:, :],
                                                    ALU.mult, ALU.add))
                link(nc.vector.tensor_tensor(tile_is[:, :, :], tile[:, :].unsqueeze(2).to_broadcast([P, NT, NS]),
                                             n.c("tile").unsqueeze(1).to_broadcast([P, NT, NS]), ALU.is_equal))
                nc.vector.tensor_tensor(tile_hi[:, :, :], tile_is[:, :, :],
                                        n.c("earlier").unsqueeze(2).to_broadcast([P, NT, NS]),
                                        ALU.mult).then_inc(tiles_found, 1)
                for q in range(0, NT, TB):
                    nc.vector.tensor_tensor(slot_is[:, q:q + TB, :],
                                            slot[:, q:q + TB].unsqueeze(2).to_broadcast([P, TB, P]),
                                            n.c("slot").unsqueeze(1).to_broadcast([P, TB, P]),
                                            ALU.is_equal).then_inc(slots_found, 1)
                link(nc.vector.tensor_tensor(first[:, :], first[:, :], ntile[:, :], ALU.add))
                link(nc.vector.tensor_tensor(te[:, :, :], first[0:1, :].unsqueeze(1).to_broadcast([1, NS, E]),
                                             n.c("tile", 1).unsqueeze(2).to_broadcast([1, NS, E]), ALU.is_le))
                link(nc.vector.reduce_sum(tef[:, :], te[:, :, :], AX.X))
                link(nc.vector.tensor_scalar(tef[:, :], tef[:, :], float(E - 1), None, ALU.min))
                link(nc.vector.tensor_copy(tile_expert[:, :], tef[:, :]))
                dve.wait_ge(numbers_done, 1)
                link(nc.vector.tensor_scalar(numf[0][:, :], psN[1][:, :], float(P), float(B * S), ALU.mult, ALU.add))
                link(nc.vector.tensor_tensor(numf[0][:, :], numf[0][:, :], psN[0][:, :], ALU.add))
                link(nc.vector.tensor_scalar(numf[1][:, :], numf[0][:, :], float(B * S - 1), None, ALU.min))
                nc.vector.tensor_copy(number[:, :], numf[0][:, :])
                nc.vector.tensor_copy(there_number[:, :], numf[1][:, :])

            @block.tensor
            def _(pe):
                def router(g):
                    pe.wait_ge(turned_copied, g + 1)
                    for k in range(4):
                        nc.tensor.matmul(psL[:, 4 * g + k, :], xT[g % 2][:, k * P:(k + 1) * P], n.wr[:, :],
                                         start=True, stop=True).then_inc(logits_done, 1)

                if r == 0:
                    pe.wait_ge(stat_done, NT)
                warm_up(nc, pe, n, psW, WARM[r])
                pe.wait_ge(n.table_loaded, 16)
                pe.wait_ge(n.router_loaded, 16 * 3)
                for g in range(NCHK):
                    if g >= 2:
                        pe.wait_ge(turned_copied, g - 1)
                    for k in range(4):
                        pe.wait_ge(normed, 4 * g + k + 1)
                        nc.tensor.transpose(psT[g % 2][:, k * P:(k + 1) * P], n.shared[:, 4 * g + k, :],
                                            n.c("ident")).then_inc(turned, 1)
                    if g >= 1:
                        router(g - 1)
                router(NCHK - 1)
                pe.wait_ge(tables_rounded, 1)
                pe.wait_ge(onehot_ready, 1)
                for k in range(NT):
                    last = nc.tensor.matmul(psC[:, :], n.onesb[:, :], onehot[:, k, :],
                                            start=(k == 0), stop=(k == NT - 1))
                last.then_inc(counts_done, 1)
                nc.tensor.matmul(psR[:, :, :], n.beforeb[:, :], onehot[:, :, :], start=True, stop=False)
                for k in range(1, NT):
                    last = nc.tensor.matmul(psR[:, k:NT, :], n.onesb[:, :], onehot[:, 0:NT - k, :],
                                            start=False, stop=(k == NT - 1))
                last.then_inc(ranks_done, 1)
                pe.wait_ge(tiles_found, 1)
                pe.wait_ge(lo_made, 1)
                for t in range(NT):
                    pe.wait_ge(slots_found, t // TB + 1)
                    nc.tensor.matmul(psN[0][:, :], slot_is[:, t, :], tile_lo[:, t, :],
                                     start=(t == 0), stop=(t == NT - 1))
                    last = nc.tensor.matmul(psN[1][:, :], slot_is[:, t, :], tile_hi[:, t, :],
                                            start=(t == 0), stop=(t == NT - 1))
                last.then_inc(numbers_done, 1)

            @block.scalar
            def _(act):
                act.wait_ge(n.table_loaded, 16)
                nc.scalar.activation(n.identb[:, :], n.c("ident"), ACT.Copy)
                nc.scalar.activation(n.beforeb[:, :], n.c("before"), ACT.Copy).then_inc(tables_rounded, 1)
                for turn in (1, 2):
                    root_of(nc, act, small[4], small[3], square_ready, root_ready, turn)
                for g in range(NCHK):
                    act.wait_ge(turned, 4 * (g + 1))
                    if g >= 2:
                        act.wait_ge(logits_done, 4 * (g - 1))
                    nc.scalar.activation(xT[g % 2][:, :], psT[g % 2][:, :], ACT.Copy).then_inc(turned_copied, 1)
                act.wait_ge(shifted, 1)
                nc.scalar.activation(lg[0][:, :, :], lg[0][:, :, :], ACT.Exp).then_inc(exp_done, 1)
                act.wait_ge(tiles_found, 1)
                nc.scalar.activation(tile_lo[:, :, :], tile_is[:, :, :], ACT.Copy,
                                     scale=n.c("partition")).then_inc(lo_made, 1)

            @block.sync
            def _(sp):
                if r == 0:
                    load_weights(sp, n)
                sp.wait_ge(rows_ready, 1)
                for b in range(B):
                    sp.dma_start(n.rows_dram[r][b * S:(b + 1) * S, :].rearrange("(n p) d -> p n d", p=P),
                                 n.tok[:, b * TB:(b + 1) * TB, :]).then_inc(rows_stored, 16)
                sp.wait_ge(rows_stored, 16 * B)
                if r == 0:
                    sp.wait_ge(n.weights_loaded, 16 * LOADS)

            if r == 0:
                @block.gpsimd
                def _(pool):
                    first_block_pool(nc, pool, n)

        with ExitStack() as ctx:
            def sem(name):
                return ctx.enter_context(nc.semaphore(f"g{r}_{name}"))

            def psum(name, width):
                return ctx.enter_context(nc.psum_tensor(f"g{r}_{name}", [P, width], F32))

            def ring(name, count, width):
                return [ctx.enter_context(nc.sbuf_tensor(f"g{r}_{name}{i}", [P, width], F32)) for i in range(count)]

            row = ring("row", LR, TW)
            xnT = ring("xnT", 2, P)
            hid, hidT = ring("hid", 2, F), ring("hidT", 2, F)
            yb, ys = ring("yb", 2, D), ring("ys", 4, D)
            w1s, w2s = ring("w1s", 4, W1W), ring("w2s", 4, W2W)
            psX, psH, psY = ([psum(f"{k}{i}", w) for i in range(2)] for k, w in (("psX", P), ("psH", F), ("psY", D)))
            psW = psum("psW", P)
            loaded = [sem(f"loaded{i}") for i in range(LR)]
            y_stored = [sem(f"y_stored{i}") for i in range(LR)]
            x_turned, x_ready, w1_ready, w2_ready, h_done, h_biased, h_ready, y_done, y_biased, y_ready = (
                sem(k) for k in ("x_turned", "x_ready", "w1_ready", "w2_ready", "h_done", "h_biased",
                                 "h_ready", "y_done", "y_biased", "y_ready"))
            block = ctx.enter_context(nc.Block())

            def run(eng, step):
                for t in range(-GATHER_AHEAD, LR):
                    step(t, t % LR)
                behind = (NS - LR) // LR * LR
                with steps(eng, LR, behind, LR) as t:
                    for k in range(LR):
                        step(t + k, k)
                for t in range(behind, NS + 3):
                    step(t, t % LR)

            def there(t):
                return not isinstance(t, int) or 0 <= t < NS

            def expert_of(eng, t):
                return eng.value_load(tile_expert[0:1, ds(t, 1)], min_val=0, max_val=E - 1)

            @block.tensor
            def _(pe):
                warm_up(nc, pe, n, psW, 12)

                def turn_x(t, k):
                    if there(t):
                        pe.wait_ge(loaded[k], (t - k) * (16 // LR) + 16)
                        wait(pe, x_ready, t - 1)
                        nc.tensor.transpose(psX[k % 2][:, :], row[k][:, D:2 * D], n.c("ident")).then_inc(x_turned, 1)

                def hidden(t, k):
                    if there(t):
                        pe.wait_ge(x_ready, t + 1)
                        pe.wait_ge(w1_ready, t + 1)
                        wait(pe, h_biased, t - 1)
                        for f in range(FB):
                            last = nc.tensor.matmul(psH[k % 2][:, f * P:(f + 1) * P], w1s[k % 4][:, f * P:(f + 1) * P],
                                                    xnT[k % 2][:, :], start=True, stop=True)
                        last.then_inc(h_done, 1)

                def result(t, k):
                    if there(t):
                        pe.wait_ge(h_ready, t + 1)
                        pe.wait_ge(w2_ready, t + 1)
                        wait(pe, y_biased, t - 1)
                        for f in range(FB):
                            last = nc.tensor.matmul(psY[k % 2][:, :], hidT[k % 2][:, f * P:(f + 1) * P],
                                                    w2s[k % 4][:, f * D:(f + 1) * D], start=(f == 0), stop=(f == FB - 1))
                        last.then_inc(y_done, 1)

                def step(t, k):
                    hidden(t, k)
                    turn_x(t + 1, (k + 1) % LR)
                    result(t - 1, (k - 1) % LR)

                run(pe, step)

            @block.scalar
            def _(act):
                def x_copy(t, k):
                    if there(t):
                        act.wait_ge(x_turned, t + 1)
                        wait(act, h_done, t - 1)
                        nc.scalar.activation(xnT[k % 2][:, :], psX[k % 2][:, :], ACT.Identity,
                                             bias=n.gb[:, 1:2], scale=n.gb[:, 0:1]).then_inc(x_ready, 1)

                def relu(t, k):
                    if there(t):
                        act.wait_ge(h_biased, t + 1)
                        wait(act, y_done, t - 1)
                        nc.scalar.activation(hidT[k % 2][:, :], hid[k % 2][:, :], ACT.Relu).then_inc(h_ready, 1)

                def second_weights(t, k):
                    if there(t):
                        e = expert_of(act, t)
                        wait(act, y_biased, t - 3)
                        nc.scalar.activation(w2s[k % 4][:, :], n.w2[:, ds(e, 1), :], ACT.Copy).then_inc(w2_ready, 1)

                def step(t, k):
                    x_copy(t + 1, (k + 1) % LR)
                    relu(t, k)
                    second_weights(t + 1, (k + 1) % LR)

                run(act, step)

            @block.vector
            def _(dve):
                def first_weights(t, k):
                    if there(t):
                        e = expert_of(dve, t)
                        wait(dve, h_done, t - 3)
                        nc.vector.tensor_copy(w1s[k % 4][:, :], n.w1[:, ds(e, 1), :]).then_inc(w1_ready, 1)

                def bias_hidden(t, k):
                    if there(t):
                        dve.wait_ge(h_done, t + 1)
                        wait(dve, h_ready, t - 1)
                        nc.vector.tensor_tensor(
                            hid[k % 2][:, :].rearrange("p (f t) -> p f t", f=FB),
                            psH[k % 2][:, :].rearrange("p (f t) -> p f t", f=FB),
                            w1s[k % 4][:, F:].unsqueeze(2).to_broadcast([P, FB, P]), ALU.add).then_inc(h_biased, 1)

                def weigh(t, k):
                    if there(t):
                        dve.wait_ge(y_done, t + 1)
                        nc.vector.tensor_tensor(yb[k % 2][:, :], psY[k % 2][:, :], w2s[k % 4][:, FB * D:],
                                                ALU.add).then_inc(y_biased, 1)

                def add_x(t, k):
                    if there(t):
                        if not (isinstance(t, int) and t < 4):
                            before = (k - 4) % LR
                            dve.wait_ge(y_stored[before], (t - 4 - before) * (16 // LR) + 16)
                        dve.wait_ge(y_biased, t + 1)
                        nc.vector.scalar_tensor_tensor(ys[k % 4][:, :], yb[k % 2][:, :], row[k][:, HALF_GATE:HALF_GATE + 1],
                                                       row[k][:, 0:D], ALU.mult, ALU.add).then_inc(y_ready, 1)

                def step(t, k):
                    bias_hidden(t, k)
                    weigh(t - 1, (k - 1) % LR)
                    first_weights(t + 2, (k + 2) % LR)
                    add_x(t - 1, (k - 1) % LR)

                run(dve, step)

            @block.gpsimd
            def _(pool):
                def gather(t, k):
                    if there(t):
                        wait(pool, y_stored[k], (t - k) * (16 // LR))
                        pool.indirect_dma_start(
                            out=row[k][:, :], out_offset=None, in_=n.rows_dram[r][:, :],
                            in_offset=bass.IndirectOffsetOnAxis(ap=there_number[:, t:t + 1],
                                                                axis=0)).then_inc(loaded[k], 16)

                def back(t, k):
                    if there(t):
                        pool.wait_ge(y_ready, t + 1)
                        pool.indirect_dma_start(
                            out=target, out_offset=bass.IndirectOffsetOnAxis(
                                ap=number[:, t:t + 1], axis=0),
                            in_=ys[k % 4][:, :], in_offset=None, bounds_check=B * S - 1,
                            oob_is_err=False).then_inc(y_stored[k], 16)


                def step(t, k):
                    gather(t + GATHER_AHEAD, (k + GATHER_AHEAD) % LR)
                    back(t - 1, (k - 1) % LR)

                for t in range(-GATHER_AHEAD, NS + 1):
                    step(t, t % LR)
                for k in range(LR):
                    pool.wait_ge(y_stored[k], 16 * ((NS - 1 - k) // LR + 1))


STACK_DMAS = 1 + KINDS * NCH


def load_stacks(sp, n, s, q, k, loaded):
    sp.dma_start(k[0:PR, :], n.k_dram[:, ds(s * QH, QH), :].rearrange("d h t -> d (h t)")
                 .unsqueeze(0).to_broadcast([KINDS, KINDS * DK, QH * S])).then_inc(loaded, 16)
    for ch in range(NCH):
        for kind in range(KINDS):
            sp.dma_start(q[kind * KINDS * DK:(kind + 1) * KINDS * DK, ch * QH * CH:(ch + 1) * QH * CH],
                         n.q_dram[kind * DK:(kind + 1) * DK, ch, ds(s * QH, QH), :]
                         .rearrange("d h t -> d (h t)").unsqueeze(0)
                         .to_broadcast([KINDS, DK, QH * CH])).then_inc(loaded, 16)


def attend(nc, n):
    with ExitStack() as ctx:
        n.prob = ctx.enter_context(nc.sbuf_tensor("prob", [P, RING, QH, CH], F32))
        n.psST = [ctx.enter_context(nc.psum_tensor(f"psST{i}", [P, CH], F32)) for i in range(3)]
        n.psS = [ctx.enter_context(nc.psum_tensor(f"psS{i}", [P, 2 * CH], F32)) for i in range(2)]
        n.rotated, n.lo_done = ([ctx.enter_context(nc.semaphore(f"p_{k}{i}")) for i in range(2)]
                                for k in ("rotated", "lo_done"))
        n.turned_copied, n.v_copied = (ctx.enter_context(nc.semaphore(f"p_{k}")) for k in ("turned_copied", "v_copied"))
        block = ctx.enter_context(nc.Block())
        project(nc, n, ctx, block)
        attention(nc, n, ctx, block)


NC8 = B * NCH


def project(nc, n, ctx, block):
    QB = H // QH
    def sb(name, shape, dt=F32):
        return ctx.enter_context(nc.sbuf_tensor(f"p_{name}", shape, dt))

    def sem(name):
        return ctx.enter_context(nc.semaphore(f"p_{name}"))

    small = [sb(f"small{i}", [P, NT]) for i in range(3)]
    an = [sb(f"an{i}", [P, CB, D]) for i in range(2)]
    anT = [sb(f"anT{i}", [P, CH]) for i in range(2)]
    rot, tmp, rest = ([[n.prob[:, m, 2 * i + k, :] for k in range(2)] for i in range(2)] for m in range(3))
    part = [[[sb(f"part{i}{k}{m}", [P, CH], BF16) for m in range(KINDS)] for k in range(2)] for i in range(2)]
    psA, psV = n.psST[0], n.psST[1]
    psP = [[n.psS[i][:, m * CH:(m + 1) * CH] for m in range(2)] for i in range(2)]
    stat_done, chain, square_ready, root_ready, normed, turned, v_done = (
        sem(k) for k in ("stat_done", "chain", "square_ready", "root_ready", "normed", "turned", "v_done"))
    proj_done, summed, hi_done, rest_done, mid_done = (
        [sem(f"{k}{i}") for i in range(2)] for k in ("proj_done", "summed", "hi_done", "rest_done", "mid_done"))
    rotated, lo_done, turned_copied, v_copied = n.rotated, n.lo_done, n.turned_copied, n.v_copied
    x_back = [sem(f"x_back{b}") for b in range(B)]
    split_stored = [[sem(f"split_stored{i}{k}") for k in range(2)] for i in range(2)]

    @block.vector
    def _(dve):
        link = Chain(dve, chain)
        token_stats(nc, dve, n, stat_done, link, x_back)
        rsqrt(nc, dve, link, n.rstd, n.var[:, :], *small, square_ready, root_ready, 1)

        def normalise(g, k):
            wait(dve, turned, g - 1)
            for j in range(CB):
                last = nc.vector.tensor_scalar(an[k][:, j, :], n.tok[:, ds(g * CB + j, 1), 0:D],
                                               n.mean[:, ds(g * CB + j, 1)], n.rstd[:, ds(g * CB + j, 1)],
                                               ALU.subtract, ALU.mult)
            last.then_inc(normed, 1)

        def rotate(g, k):
            for i in range(2):
                dve.wait_ge(proj_done[i], g + 1)
                wait(dve, rest_done[i], g - 1)
                nc.vector.tensor_tensor(rot[i][k][:, :], psP[i][0][:, :], n.c("cos")[:, k * CH:(k + 1) * CH],
                                        ALU.mult)
                nc.vector.tensor_tensor(tmp[i][k][:, :], psP[i][1][:, :], n.c("sin")[:, k * CH:(k + 1) * CH],
                                        ALU.mult).then_inc(rotated[i], 1)

        def subtract_hi(g, k):
            for i in range(2):
                dve.wait_ge(hi_done[i], g + 1)
                wait(dve, lo_done[i], g - 1)
                nc.vector.tensor_tensor(rest[i][k][:, :], rot[i][k][:, :], part[i][k][0][:, :],
                                        ALU.subtract).then_inc(rest_done[i], 1)

        normalise(0, 0)
        normalise(1, 1)
        normalise(2, 0)
        rotate(0, 0)
        normalise(3, 1)
        rotate(1, 1)
        subtract_hi(0, 0)
        with steps(dve, 2, NC8 - 2, 2) as g:
            normalise(g + 2, 0)
            rotate(g, 0)
            subtract_hi(g - 1, 1)
            normalise(g + 3, 1)
            rotate(g + 1, 1)
            subtract_hi(g, 0)
        rotate(NC8 - 2, 0)
        subtract_hi(NC8 - 3, 1)
        rotate(NC8 - 1, 1)
        subtract_hi(NC8 - 2, 0)
        subtract_hi(NC8 - 1, 1)

    @block.tensor
    def _(pe):
        def turn(g, k):
            pe.wait_ge(normed, g + 1)
            wait(pe, turned_copied, g)
            for j in range(CB):
                last = nc.tensor.transpose(psA[:, j * P:(j + 1) * P], an[k][:, j, :], n.c("ident"))
            last.then_inc(turned, 1)

        def products(g, k):
            pe.wait_ge(turned_copied, g + 1)
            for i in range(2):
                wait(pe, rotated[i], g)
                for m in range(2):
                    last = nc.tensor.matmul(psP[i][m][:, :], n.wproj[:, 2 * i + m, :], anT[k][:, :],
                                            start=True, stop=True)
                last.then_inc(proj_done[i], 1)
            wait(pe, v_copied, g)
            for j in range(CB):
                last = nc.tensor.matmul(psV[:, j * P:(j + 1) * P], anT[k][:, j * P:(j + 1) * P],
                                        n.wproj[:, 4, :], start=True, stop=True)
            last.then_inc(v_done, 1)

        turn(0, 0)
        turn(1, 1)
        products(0, 0)
        with steps(pe, 0, NC8 - 2, 2) as g:
            turn(g + 2, 0)
            products(g + 1, 1)
            turn(g + 3, 1)
            products(g + 2, 0)
        products(NC8 - 1, 1)

    @block.scalar
    def _(act):
        root_of(nc, act, small[1], small[0], square_ready, root_ready, 1)

        def copy_turned(g, k):
            act.wait_ge(turned, g + 1)
            wait(act, v_done, g - 1)
            nc.scalar.activation(anT[k][:, :], psA[:, :], ACT.Copy).then_inc(turned_copied, 1)

        def values(g, k):
            act.wait_ge(v_done, g + 1)
            nc.scalar.activation(n.vals[:, ds((g - k) * 2, QB), k * CB:(k + 1) * CB, :],
                                 psV[:, :].rearrange("p (j q r) -> p q j r", j=CB, q=QB),
                                 ACT.Copy).then_inc(v_copied, 1)

        def hi(g, k):
            for i in range(2):
                act.wait_ge(summed[i], g + 1)
                wait(act, split_stored[i][k], 16 * KINDS // 2 * (g - k))
                nc.scalar.activation(part[i][k][0][:, :], rot[i][k][:, :], ACT.Copy).then_inc(hi_done[i], 1)

        def mid(g, k):
            for i in range(2):
                act.wait_ge(rest_done[i], g + 1)
                nc.scalar.activation(part[i][k][1][:, :], rest[i][k][:, :], ACT.Copy).then_inc(mid_done[i], 1)

        copy_turned(0, 0)
        copy_turned(1, 1)
        values(0, 0)
        copy_turned(2, 0)
        hi(0, 0)
        values(1, 1)
        copy_turned(3, 1)
        mid(0, 0)
        hi(1, 1)
        with steps(act, 2, NC8 - 2, 2) as g:
            values(g, 0)
            copy_turned(g + 2, 0)
            mid(g - 1, 1)
            hi(g, 0)
            values(g + 1, 1)
            copy_turned(g + 3, 1)
            mid(g, 0)
            hi(g + 1, 1)
        values(NC8 - 2, 0)
        mid(NC8 - 3, 1)
        hi(NC8 - 2, 0)
        values(NC8 - 1, 1)
        mid(NC8 - 2, 0)
        hi(NC8 - 1, 1)
        mid(NC8 - 1, 1)

    @block.gpsimd
    def _(pool):
        def add_pairs(g, k):
            for i in range(2):
                pool.wait_ge(rotated[i], g + 1)
                nc.gpsimd.tensor_tensor(rot[i][k][:, :], rot[i][k][:, :], tmp[i][k][:, :],
                                        ALU.add).then_inc(summed[i], 1)

        def subtract_mid(g, k):
            for i in range(2):
                pool.wait_ge(mid_done[i], g + 1)
                nc.gpsimd.tensor_tensor(part[i][k][2][:, :], rest[i][k][:, :], part[i][k][1][:, :],
                                        ALU.subtract).then_inc(lo_done[i], 1)

        add_pairs(0, 0)
        add_pairs(1, 1)
        with steps(pool, 2, NC8, 2) as g:
            for k in range(2):
                subtract_mid(g - 2 + k, k)
                add_pairs(g + k, k)
        subtract_mid(NC8 - 2, 0)
        subtract_mid(NC8 - 1, 1)

    @block.sync
    def _(sp):
        for b in range(B):
            sp.dma_start(n.tok[:, b * TB:(b + 1) * TB, 0:D],
                         n.x_dram[b * S:(b + 1) * S, :].rearrange("(n p) d -> p n d", p=P)).then_inc(x_back[b], 16)
        def keep(g):
            for k in range(2):
                for i in range(2):
                    sp.wait_ge(lo_done[i], g + k + 1)
                    for m in range(KINDS):
                        rows = slice(m * DK, (m + 1) * DK)
                        if i == 0:
                            there = n.q_dram[rows, k, ds(g * (H // 2), H), :]
                        else:
                            there = n.k_dram[rows, ds(g * (H // 2), H), k * CH:(k + 1) * CH]
                        sp.dma_start(there.rearrange("d h t -> h d t"),
                                     part[i][k][m][:, :]).then_inc(split_stored[i][k], 16)

        with steps(sp, 0, NC8 - 2, 2) as g:
            keep(g)
        load_stacks(sp, n, 0, n.qs[0], n.ks[0], n.first_stack_loaded)
        keep(NC8 - 2)
        for i in range(2):
            for k in range(2):
                sp.wait_ge(split_stored[i][k], 16 * KINDS * NC8 // 2)


def attention(nc, n, ctx, block):
    units = []
    for ch in range(NCH):
        for j in range((ch + 1) * CB):
            q0 = max(j * P, ch * CH)
            units.append((ch, j, q0, (ch + 1) * CH - q0))
    UN = len(units)
    SC = UN * QH
    diagonal = [u for u, (ch, j, q0, w) in enumerate(units) if j * P == q0]
    half_start = [0, CB]
    half_end = [CB, UN]
    tiles = [((h, h + 1), i) for i in range(CB) for h in range(0, QH, 2)]
    HALF_TILES = len(tiles)
    tiles += [((h,), i) for i in (CB, TB - 1, CB + 1, TB - 2) for h in range(QH)]
    MT = len(tiles)

    tile_cost = [len(heads) * (i + 1) * P + 350 for heads, i in tiles]
    tile_total = sum(tile_cost)
    WEIGH_COST = 3
    att_total = sum((QH + WEIGH_COST) * w for _, _, _, w in units)

    def plan(first, last):
        found, att, tile = [], 0, 0

        def spread():
            nonlocal tile
            while not last and tile < MT and sum(tile_cost[:tile + 1]) * att_total <= att * tile_total + AHEAD:
                found.append(("tile", tile, 0))
                tile += 1

        for u in range(UN):
            w = units[u][3]
            for h in range(QH):
                found.append(("score", u, h))
                att += w
                if h == 0:
                    if u >= LAG:
                        found.append(("weigh", u - LAG, 0))
                        att += WEIGH_COST * units[u - LAG][3]
                    elif not first:
                        found.append(("weigh", u - LAG, 1))
                        att += WEIGH_COST * units[u - LAG + UN][3]
                spread()
            for at, what, arg, there in EXTRAS:
                if at == u and (there or not (first if arg == 1 and what == "turn_out" else last)):
                    found.append((what, arg, 0))
        att = att_total * 2
        spread()
        return found

    def uses(first, last):
        return [(0, what, arg) for what, arg, _ in plan(first, last) if what in ("tile", "turn_max", "turn_out")]

    LAG = 2
    AHEAD = tile_total * tile_cost[0]
    EXTRAS = [(1, "turn_max", 1, True), (4, "turn_out", 1, False), (5, "turn_out", 0, True),
              (7, "turn_max", 0, False)]
    before_loop = [(0, "tile", t) for t in range(MT // 2)] + [(0, "turn_max", 0)]
    before_loop += [(0, "tile", t) for t in range(MT // 2, MT)]
    USES = len(uses(False, False))

    def base(s, first):
        return len(before_loop) if first else len(before_loop) + len(uses(True, False)) + (s - 1) * USES

    PARITY = base(1, False) % 2
    assert USES % 2 == 0

    def q_col(h, q):
        return (q // CH * QH + h) * CH + q % CH

    def sb(name, shape, dt=F32):
        return ctx.enter_context(nc.sbuf_tensor(f"a_{name}", shape, dt))

    def psum(name, width):
        return ctx.enter_context(nc.psum_tensor(f"a_{name}", [P, width], F32))

    def sem(name):
        return ctx.enter_context(nc.semaphore(f"a_{name}"))

    qs = n.qs + [sb(f"qs{i}", [PR + MR, QH * S], BF16) for i in range(1, RING)]
    ks, vs = n.ks, n.vs
    MP = KINDS * QH * CB
    prob, psST, psS = n.prob, n.psST, n.psS
    rowmax = sb("rowmax", [P, QH, TB])
    maxparts = sb("maxparts", [P, P], BF16)
    maxrest = [sb(f"maxrest{i}", [P, QH, CB]) for i in range(2)]
    maxT = [sb(f"maxT{i}", [MP, P], BF16) for i in range(2)]
    zeros = sb("zeros", [P, QH, CB])
    gate = sb("gate", [1, UN])
    outT = sb("outT", [P, CH])
    recip = [sb(f"recip{i}", [P, CB, QH]) for i in range(NCH)]
    psO = psum("psO", CH)
    maxpart = maxparts[:, 0:MP].rearrange("p (k h i) -> p k h i", k=KINDS, h=QH)
    QB = H // QH

    (cleared, v_ready, scored, use_done, use_read, exp_done, masked, pv_done, out_copied, split_done,
     maxT_ready, split_chain, out_read) = (sem(k) for k in (
         "cleared", "v_ready", "scored", "use_done", "use_read", "exp_done", "masked", "pv_done",
         "out_copied", "split_done", "maxT_ready", "split_chain", "out_read"))
    stack_loaded = [n.first_stack_loaded] + [sem(f"stack_loaded{i}") for i in range(1, RING)]
    max_loaded = [sem(f"max_loaded{i}") for i in range(2)]

    def run(eng, stage):
        stage(0, 0, 0, True, False)
        with eng.Fori(0, (NST - 4) // RING) as i:
            for k in range(1, RING + 1):
                stage(i * RING + k, k % RING, i + k // RING, False, False)
        for s in range(NST - RING, NST):
            stage(s, s % RING, s // RING, False, s == NST - 1)

    @block.sync
    def _(sp):
        def load(s, r):
            wait(sp, scored, (s - RING + 1) * SC)
            load_stacks(sp, n, s, qs[r], ks[r], stack_loaded[r])

        def load_max(s, r, half):
            sp.wait_ge(maxT_ready, 2 * s + half + 1)
            sp.dma_start(qs[r][PR:PR + MR, half * QH * CH:(half + 1) * QH * CH],
                         maxT[half][:, :]).then_inc(max_loaded[half], 16)

        def stage(s, r, turn, first, last):
            if not first and not last and not (isinstance(s, int) and s + 2 >= NST):
                load(s + 2, (r + 2) % RING)
            load_max(s, r, 1)
            if not last:
                load_max(s + 1, (r + 1) % RING, 0)

        load(1, 1)
        load_max(0, 0, 0)
        load(2, 2)
        run(sp, stage)

    @block.tensor
    def _(pe):
        def use(index):
            wait(pe, use_read, index - 1)

        def tile(r, turn, t, index, ps):
            heads, i = tiles[t]
            if t == 0:
                pe.wait_ge(stack_loaded[r], (turn + 1) * 16 * STACK_DMAS)
            use(index)
            width = (i + 1) * P
            for a, h in enumerate(heads):
                lhs = qs[r][0:PR, q_col(h, i * P):q_col(h, i * P) + P]
                for c0 in range(0, width, CH):
                    w = min(CH, width - c0)
                    nc.tensor.matmul(ps[:, a * CH + c0:a * CH + c0 + w], lhs,
                                     ks[r][0:PR, h * S + c0:h * S + c0 + w], start=True, stop=c0 + w < width)
                last = nc.tensor.matmul(ps[:, a * CH + i * P:a * CH + width], n.identb[:, :], n.maskb[:, :],
                                        start=False, stop=True)
            last.then_inc(use_done, 1)

        def turn_max(s, half, index, ps):
            use(index)
            pe.wait_ge(split_done, 2 * s + half + 1)
            nc.tensor.transpose(ps[:, 0:P // 2].bitcast(BF16), maxparts[:, :], n.identb[:, :]).then_inc(use_done, 1)

        def turn_out(s, ch, index, ps):
            use(index)
            pe.wait_ge(out_copied, 2 * s + ch + 1)
            for b in range(CB):
                last = nc.tensor.transpose(ps[:, b * P:(b + 1) * P], outT[:, b * P:(b + 1) * P], n.c("ident"))
            last.then_inc(use_done, 1)

        def score(s, r, u, h):
            ch, j, q0, w = units[u]
            if u in half_start and h == 0:
                half = half_start.index(u)
                pe.wait_ge(max_loaded[half], (s + 1) * 16)
            wait(pe, exp_done, s * SC + u * QH + h - 2)
            nc.tensor.matmul(psST[(u * QH + h) % 3][:, 0:w], ks[r][:, h * S + j * P:h * S + (j + 1) * P],
                             qs[r][:, q_col(h, q0):q_col(h, q0) + w], start=True, stop=True).then_inc(scored, 1)

        def weigh(s, r, u):
            ch, j, q0, w = units[u]
            pe.wait_ge(exp_done, s * SC + (u + 1) * QH)
            if u in diagonal:
                pe.wait_ge(masked, s * len(diagonal) + diagonal.index(u) + 1)
            if u in half_start:
                pe.wait_ge(v_ready, s + 1)
                wait(pe, out_copied, 2 * s + half_start.index(u))
            c0 = q0 - ch * CH
            for h in range(QH):
                last = nc.tensor.matmul(psO[32 * h:32 * h + 32, c0:c0 + w], vs[r][:, j, h, :],
                                        prob[:, u % RING, h, 0:w], start=(j == 0),
                                        stop=(u + 1 in half_end))
            last.then_inc(pv_done, 1)

        def stage(s, r, turn, first, last):
            b, parity = base(s, first), base(0, True) % 2 if first else PARITY
            k = 0
            for what, arg, arg2 in plan(first, last):
                if what == "score":
                    score(s, r, arg, arg2)
                    continue
                if what == "weigh":
                    if arg2:
                        weigh(s - 1, (r - 1) % RING, arg + UN)
                    else:
                        weigh(s, r, arg)
                    continue
                ps = psS[(parity + k) % 2]
                if what == "tile":
                    tile((r + 1) % RING, turn + (r + 1) // RING, arg, b + k, ps)
                elif what == "turn_max":
                    turn_max(s if arg else s + 1, arg, b + k, ps)
                else:
                    turn_out(s - 1 if arg else s, arg, b + k, ps)
                k += 1

        for i in range(2):
            pe.wait_ge(n.rotated[i], NC8)
        pe.wait_ge(n.turned_copied, NC8)
        pe.wait_ge(n.v_copied, NC8)
        for k, (_, what, arg) in enumerate(before_loop):
            if what == "tile":
                tile(0, 0, arg, k, psS[k % 2])
            else:
                turn_max(0, arg, k, psS[k % 2])
        run(pe, stage)
        weigh(NST - 1, (NST - 1) % RING, UN - 2)
        weigh(NST - 1, (NST - 1) % RING, UN - 1)
        end = base(NST - 1, False) + len(uses(False, True))
        turn_out(NST - 1, 1, end, psS[end % 2])

    @block.scalar
    def _(act):
        def exps(s, u):
            ch, j, q0, w = units[u]
            wait(act, pv_done, s * UN + u - 2)
            for h in range(QH):
                act.wait_ge(scored, s * SC + u * QH + h + 1)
                nc.scalar.activation(prob[:, u % RING, h, 0:w], psST[(u * QH + h) % 3][:, 0:w], ACT.Exp,
                                     scale=SCALE).then_inc(exp_done, 1)

        def copy_out(s, ch):
            act.wait_ge(pv_done, s * UN + half_end[ch])
            wait(act, out_read, 2 * s + ch)
            nc.scalar.activation(outT[:, :], psO[:, :], ACT.Copy).then_inc(out_copied, 1)

        def stage(s, r, turn, first, last):
            for u in range(UN):
                if u == 1 and not first:
                    copy_out(s - 1, 1)
                if u == half_end[0] + 1:
                    copy_out(s, 0)
                exps(s, u)

        for i in range(2):
            act.wait_ge(n.lo_done[i], NC8)
        run(act, stage)
        copy_out(NST - 1, 1)

    @block.vector
    def _(dve):
        nc.vector.memset(maxparts[:, :], 0.0)
        nc.vector.memset(zeros[:, :, :], 0.0).then_inc(cleared, 1)

        def reduce(s, t, index, ps):
            heads, i = tiles[t]
            if t in (0, HALF_TILES):
                wait(dve, split_done, 2 * s - 1 + (t > 0))
            dve.wait_ge(use_done, index + 1)
            width = (i + 1) * P
            if len(heads) == 2:
                src = ps[:, :].rearrange("p (a c) -> p a c", a=2)[:, :, 0:width]
                nc.vector.reduce_max(rowmax[:, heads[0]:heads[0] + 2, i], src, AX.X).then_inc(use_read, 1)
            else:
                nc.vector.reduce_max(rowmax[:, heads[0]:heads[0] + 1, i], ps[:, 0:width],
                                     AX.X).then_inc(use_read, 1)

        def copy_max(s, half, index, ps):
            dve.wait_ge(use_done, index + 1)
            wait(dve, max_loaded[half], s * 16)
            nc.vector.tensor_copy(maxT[half][:, :],
                                  ps[0:MP, 0:P // 2].bitcast(BF16)).then_inc(use_read, 1)
            dve.wait_ge(use_read, index + 1)
            dve.sem_inc(maxT_ready, 1)

        def normalise(s, ch, index, ps):
            dve.wait_ge(use_done, index + 1)
            src = ps[:, 0:CH].rearrange("p (b h c) -> p b h c", b=CB, h=QH)
            nc.vector.reciprocal(recip[ch][:, :, :], src[:, :, :, DK]).then_inc(out_read, 1)
            dve.wait_ge(out_read, 2 * s + ch + 1)
            nc.vector.tensor_tensor(
                n.shared[:, ds((s // QB) * TB + ch * CB, CB), ds((s % QB) * RW, RW)]
                .rearrange("p j (h d) -> p j h d", h=QH),
                src[:, :, :, 0:DK], recip[ch][:, :, :].unsqueeze(3).to_broadcast([P, CB, QH, DK]),
                ALU.mult).then_inc(use_read, 1)

        def do(s, what, arg, index, ps):
            if what == "tile":
                reduce(s + 1, arg, index, ps)
            elif what == "turn_max":
                copy_max(s if arg else s + 1, arg, index, ps)
            else:
                normalise(s - 1 if arg else s, arg, index, ps)

        def stage(s, r, turn, first, last):
            b, parity = base(s, first), base(0, True) % 2 if first else PARITY
            for k, (_, what, arg) in enumerate(uses(first, last)):
                do(s, what, arg, b + k, psS[(parity + k) % 2])

        for k, (_, what, arg) in enumerate(before_loop):
            do(-1, what, arg, k, psS[k % 2])
        run(dve, stage)
        end = base(NST - 1, False) + len(uses(False, True))
        normalise(NST - 1, 1, end, psS[end % 2])

    @block.gpsimd
    def _(pool):
        half_ready = {}
        for what, found in (("first", uses(True, False)), ("middle", uses(False, False))):
            for half, t in ((0, HALF_TILES - 1), (1, MT - 1)):
                half_ready[what, half] = [k for k, (_, w, a) in enumerate(found) if (w, a) == ("tile", t)][0] + 1
        def split(s, half, count, order):
            pool.wait_ge(use_read, count)
            wait(pool, maxT_ready, 2 * s + half)
            src = rowmax[:, :, half * CB:(half + 1) * CB]
            done = order * 4

            def link(ins, k):
                ins.then_inc(split_chain, 1)
                pool.wait_ge(split_chain, done + k)

            zero = zeros[:, :, :]
            link(nc.gpsimd.tensor_tensor(maxpart[:, 0, :, :], zero, src, ALU.subtract), 1)
            link(nc.gpsimd.tensor_tensor(maxrest[0][:, :, :], src, maxpart[:, 0, :, :], ALU.add), 2)
            link(nc.gpsimd.tensor_tensor(maxpart[:, 1, :, :], zero, maxrest[0][:, :, :], ALU.subtract), 3)
            link(nc.gpsimd.tensor_tensor(maxrest[1][:, :, :], maxrest[0][:, :, :], maxpart[:, 1, :, :],
                                         ALU.add), 4)
            nc.gpsimd.tensor_tensor(maxpart[:, 2, :, :], zero, maxrest[1][:, :, :],
                                    ALU.subtract).then_inc(split_done, 1)

        def values(s, r):
            wait(pool, pv_done, (s - RING + 1) * UN + 1)
            nc.gpsimd.tensor_copy(vs[r][:, :, :, 0:DK],
                                  n.vals[:, ds(s, 1), :, :].rearrange("p s j (h d) -> p (s j) h d", h=QH)
                                  ).then_inc(v_ready, 1)

        def mask(s, u):
            pool.wait_ge(exp_done, s * SC + (u + 1) * QH)
            part = prob[:, u % RING, :, 0:P]
            nc.gpsimd.tensor_tensor(gate[:, u:u + 1], zeros[0:1, 0, 0:1], zeros[0:1, 0, 1:2], ALU.add)
            nc.gpsimd.affine_select(out=part, in_=part, compare_op=ALU.is_ge, fill=0.0, base=0,
                                    pattern=[[0, QH], [1, P]], channel_multiplier=-1).then_inc(masked, 1)

        def stage(s, r, turn, first, last):
            for u in diagonal:
                if u == half_end[0] + CB:
                    if not last:
                        split(s + 1, 0, base(s, first) + half_ready["first" if first else "middle", 0],
                              2 * s + 2)
                        values(s + 1, (r + 1) % RING)
                mask(s, u)
            if not last:
                split(s + 1, 1, base(s, first) + half_ready["first" if first else "middle", 1], 2 * s + 3)

        pool.wait_ge(cleared, 1)
        pool.wait_ge(n.v_copied, NC8)
        nc.gpsimd.tensor_copy(vs[0][:, :, :, 0:DK],
                              n.vals[:, 0, :, :].rearrange("p j (h d) -> p j h d", h=QH)).then_inc(v_ready, 1)
        split(0, 0, HALF_TILES, 0)
        split(0, 1, len(before_loop), 1)
        run(pool, stage)


def output_projection(nc, n):
    QB = H // QH
    G = NT // CB
    with ExitStack() as ctx:
        oT = [ctx.enter_context(nc.sbuf_tensor(f"o_T{i}", [P, CH], F32)) for i in range(2)]
        psT = [ctx.enter_context(nc.psum_tensor(f"o_psT{i}", [P, CH], F32)) for i in range(2)]
        psY = [ctx.enter_context(nc.psum_tensor(f"o_psY{i}", [P, CH], F32)) for i in range(2)]
        turned, turned_copied, projected, added = (ctx.enter_context(nc.semaphore(f"o_{k}")) for k in (
            "turned", "turned_copied", "projected", "added"))
        block = ctx.enter_context(nc.Block())

        @block.tensor
        def _(pe):
            def product(g):
                pe.wait_ge(turned_copied, g + 1)
                wait(pe, added, g - 1)
                for j in range(CB):
                    last = nc.tensor.matmul(psY[g % 2][:, j * P:(j + 1) * P], oT[g % 2][:, j * P:(j + 1) * P],
                                            n.wproj[:, 5, :], start=True, stop=True)
                last.then_inc(projected, 1)

            for g in range(G):
                wait(pe, turned_copied, g - 1)
                for j in range(CB):
                    last = nc.tensor.transpose(psT[g % 2][:, j * P:(j + 1) * P],
                                               n.shared[:, g * CB + j, :], n.c("ident"))
                last.then_inc(turned, 1)
                if g >= 1:
                    product(g - 1)
            product(G - 1)

        @block.scalar
        def _(act):
            for g in range(G):
                act.wait_ge(turned, g + 1)
                wait(act, projected, g - 1)
                nc.scalar.activation(oT[g % 2][:, :], psT[g % 2][:, :], ACT.Copy).then_inc(turned_copied, 1)

        @block.vector
        def _(dve):
            def measure(g):
                dve.wait_ge(added, g + 1)
                for t in range(g * CB, (g + 1) * CB):
                    nc.vector.bn_stats(n.stats[:, t, :], n.tok[:, t, 0:D])

            for g in range(G):
                dve.wait_ge(projected, g + 1)
                part = n.tok[:, g * CB:(g + 1) * CB, 0:D]
                nc.vector.tensor_tensor(part, part, psY[g % 2][:, :].rearrange("p (j d) -> p j d", j=CB),
                                        ALU.add).then_inc(added, 1)
                if g >= 1:
                    measure(g - 1)
            measure(G - 1)


_OUT = (B, S, D)


def kernel(**inputs):
    import concourse.bacc as bacc
    from concourse.bass_utils import run_bass_kernel_spmd

    def arr(name):
        return np.ascontiguousarray(inputs[name])

    def swapped(w):
        return w.reshape(D // 2, 2, D)[:, ::-1, :].reshape(D, D)

    wq, wk = arr("L0_attn_Wq"), arr("L0_attn_Wk")
    weights = (wq, swapped(wq), wk, swapped(wk), arr("L0_attn_Wv"), arr("L0_attn_Wo"))
    arrays = {
        "x": arr("L0_attn_x"), "Wp": np.stack([w.T for w in weights], axis=1),
        "Wr": arr("L0_ffn_Wr"), "br": arr("L0_ffn_br"),
        "ln": np.stack([arr("L0_ffn_ln_g"), arr("L0_ffn_ln_b")], axis=1),
        "Wb1": np.concatenate([arr("L0_ffn_W1").transpose(1, 0, 2),
                               arr("L0_ffn_b1").reshape(E, FB, P).transpose(2, 0, 1)], axis=2),
        "W2": np.ascontiguousarray(arr("L0_ffn_W2").reshape(E, FB, P, D).transpose(2, 0, 1, 3).reshape(P, E, FB * D)),
        "b2": arr("L0_ffn_b2"), "const": constants(),
    }
    nc = bacc.Bacc("TRN2", target_bir_lowering=False, num_devices=1)
    args = {k: nc.dram_tensor(f"in_{k}", a.shape, mybir.dt.from_np(a.dtype), kind="ExternalInput").ap()
            for k, a in arrays.items()}
    out = nc.dram_tensor("out_x", _OUT, F32, kind="ExternalOutput").ap()
    build(nc, out=out, **args)
    result = run_bass_kernel_spmd(nc, [{f"in_{k}": a for k, a in arrays.items()}], core_ids=[0])
    return result.results[0]["out_x"]
```
